# Optimizing a Trainium2 kernel written in Bass

```python
import numpy as np
import jax
import jax.numpy as jnp

def _softmax(x, axis=-1):
    return jax.nn.softmax(x, axis=axis)

def _gelu(x):
    return jax.nn.gelu(x, approximate=True)

def _silu(x):
    return jax.nn.silu(x)

def _sigmoid(x):
    return jax.nn.sigmoid(x)

def _layernorm(x, axis=-1, eps=1e-05):
    m = jnp.mean(x, axis=axis, keepdims=True)
    v = jnp.var(x, axis=axis, keepdims=True)
    return (x - m) / jnp.sqrt(v + eps)

def _scatter_add(tgt, idx, src, axis=0):
    return tgt.at[idx].add(src)

def _segment_sum(src, seg, n):
    return jax.ops.segment_sum(src, seg, n)
kernel_name = 'mk_conv_seq_d4_conv_nchw256_r4_36d872'

def setup_inputs(seed: int=0):
    np.random.seed(seed)
    _w = jnp.asarray

    def _rec_inputs():
        import jax
        import jax.numpy as jnp
        _gk = jax.random.key(seed)
        x = -0.0002928 + 1 * jax.random.normal(jax.random.fold_in(_gk, 1), (4, 64, 16, 16), jnp.float32)
        return x
    x = _rec_inputs()

    def _L0_conv_setup():
        import jax, jax.numpy as jnp
        import numpy as np
        B, C, HID, H, W = (4, 64, 32, 16, 16)
        key = jax.random.key(seed)
        ks = jax.random.split(key, 7)
        x = jax.random.normal(ks[0], (B, C, H, W), dtype=jnp.float32)
        Wq = jax.random.normal(ks[1], (HID, C), dtype=jnp.float32) * 0.02
        bq = jax.random.normal(ks[2], (HID,), dtype=jnp.float32) * 0.02
        Wk = jax.random.normal(ks[3], (HID, C), dtype=jnp.float32) * 0.02
        bk = jax.random.normal(ks[4], (HID,), dtype=jnp.float32) * 0.02
        Wv = jax.random.normal(ks[5], (C, C), dtype=jnp.float32) * 0.02
        bv = jax.random.normal(ks[6], (C,), dtype=jnp.float32) * 0.02
        return {'x': x, 'Wq': Wq, 'bq': bq, 'Wk': Wk, 'bk': bk, 'Wv': Wv, 'bv': bv}
    _L0_conv_all = _L0_conv_setup()
    _L0_conv_in = {k: v for k, v in _L0_conv_all.items() if k in ('Wq', 'bq', 'Wk', 'bk', 'Wv', 'bv')}
    del _L0_conv_all

    def _L1_conv_setup():
        import jax, jax.numpy as jnp
        import numpy as np
        key = jax.random.key(seed)
        ks = jax.random.split(key, 8)
        B, C, W, H = (4, 64, 16, 16)
        Ck = C // 8
        x = jax.random.normal(ks[0], (B, C, W, H), dtype=jnp.float32)
        sf = (6.0 / (C + Ck)) ** 0.5
        sh = (6.0 / (C + C)) ** 0.5
        Wf = jax.random.uniform(ks[1], (Ck, C), jnp.float32, -sf, sf)
        Wg = jax.random.uniform(ks[2], (Ck, C), jnp.float32, -sf, sf)
        Wh = jax.random.uniform(ks[3], (C, C), jnp.float32, -sh, sh)
        bf = jnp.zeros((Ck,), jnp.float32)
        bg = jnp.zeros((Ck,), jnp.float32)
        bh = jnp.zeros((C,), jnp.float32)
        gamma = jax.random.uniform(ks[4], (1,), jnp.float32) * 0.5
        return {'x': x, 'Wf': Wf, 'bf': bf, 'Wg': Wg, 'bg': bg, 'Wh': Wh, 'bh': bh, 'gamma': gamma}
    _L1_conv_all = _L1_conv_setup()
    _L1_conv_in = {k: v for k, v in _L1_conv_all.items() if k in ('Wf', 'bf', 'Wg', 'bg', 'Wh', 'bh', 'gamma')}
    del _L1_conv_all

    def _L2_conv_setup():
        import jax, jax.numpy as jnp
        import numpy as np
        key = jax.random.key(seed)
        kx, kq, kk, kv = jax.random.split(key, 4)
        B, C, H, W = (4, 64, 16, 16)
        scale = 1.0 / np.sqrt(C)
        return {'x': jax.random.normal(kx, (B, C, H, W), dtype=jnp.float32), 'Wq': jax.random.normal(kq, (C, C), dtype=jnp.float32) * scale, 'Wk': jax.random.normal(kk, (C, C), dtype=jnp.float32) * scale, 'Wv': jax.random.normal(kv, (C, C), dtype=jnp.float32) * scale, 'gamma': jnp.ones((1,), dtype=jnp.float32) * 0.1}
    _L2_conv_all = _L2_conv_setup()
    _L2_conv_in = {k: v for k, v in _L2_conv_all.items() if k in ('Wq', 'Wk', 'Wv', 'gamma')}
    del _L2_conv_all

    def _L3_conv_setup():
        import jax, jax.numpy as jnp
        import numpy as np
        CHANNELS = 64
        HEADS = 8
        GROUPS = 32
        EPS = 1e-05
        key = jax.random.key(seed)
        ks = jax.random.split(key, 9)
        c = CHANNELS
        s = 1.0 / np.sqrt(c)
        return {'x': jax.random.normal(ks[0], (2, c, 16, 16), dtype=jnp.float32), 'gn_w': jnp.ones((c,), jnp.float32), 'gn_b': jnp.zeros((c,), jnp.float32), 'qkv_w': jax.random.normal(ks[1], (3 * c, c), jnp.float32) * s, 'qkv_b': jnp.zeros((3 * c,), jnp.float32), 'proj_w': jax.random.normal(ks[2], (c, c), jnp.float32) * s, 'proj_b': jnp.zeros((c,), jnp.float32), 'gproj_w': jax.random.normal(ks[3], (c, c), jnp.float32) * s, 'gproj_b': jnp.zeros((c,), jnp.float32)}
    _L3_conv_all = _L3_conv_setup()
    _L3_conv_in = {k: v for k, v in _L3_conv_all.items() if k in ('gn_w', 'gn_b', 'qkv_w', 'qkv_b', 'proj_w', 'proj_b', 'gproj_w', 'gproj_b')}
    del _L3_conv_all
    return {'x': x, 'L0_conv_Wq': _L0_conv_in['Wq'], 'L0_conv_bq': _L0_conv_in['bq'], 'L0_conv_Wk': _L0_conv_in['Wk'], 'L0_conv_bk': _L0_conv_in['bk'], 'L0_conv_Wv': _L0_conv_in['Wv'], 'L0_conv_bv': _L0_conv_in['bv'], 'L1_conv_Wf': _L1_conv_in['Wf'], 'L1_conv_bf': _L1_conv_in['bf'], 'L1_conv_Wg': _L1_conv_in['Wg'], 'L1_conv_bg': _L1_conv_in['bg'], 'L1_conv_Wh': _L1_conv_in['Wh'], 'L1_conv_bh': _L1_conv_in['bh'], 'L1_conv_gamma': _L1_conv_in['gamma'], 'L2_conv_Wq': _L2_conv_in['Wq'], 'L2_conv_Wk': _L2_conv_in['Wk'], 'L2_conv_Wv': _L2_conv_in['Wv'], 'L2_conv_gamma': _L2_conv_in['gamma'], 'L3_conv_gn_w': _L3_conv_in['gn_w'], 'L3_conv_gn_b': _L3_conv_in['gn_b'], 'L3_conv_qkv_w': _L3_conv_in['qkv_w'], 'L3_conv_qkv_b': _L3_conv_in['qkv_b'], 'L3_conv_proj_w': _L3_conv_in['proj_w'], 'L3_conv_proj_b': _L3_conv_in['proj_b'], 'L3_conv_gproj_w': _L3_conv_in['gproj_w'], 'L3_conv_gproj_b': _L3_conv_in['gproj_b']}

def reference(x, L0_conv_Wq, L0_conv_bq, L0_conv_Wk, L0_conv_bk, L0_conv_Wv, L0_conv_bv, L1_conv_Wf, L1_conv_bf, L1_conv_Wg, L1_conv_bg, L1_conv_Wh, L1_conv_bh, L1_conv_gamma, L2_conv_Wq, L2_conv_Wk, L2_conv_Wv, L2_conv_gamma, L3_conv_gn_w, L3_conv_gn_b, L3_conv_qkv_w, L3_conv_qkv_b, L3_conv_proj_w, L3_conv_proj_b, L3_conv_gproj_w, L3_conv_gproj_b):
    import jax
    import jax.numpy as jnp

    def _L0_conv_ref(x, Wq, bq, Wk, bk, Wv, bv):
        import jax, jax.numpy as jnp
        import numpy as np
        B, C, HID, H, W = (4, 64, 32, 16, 16)
        b, c, h, w = x.shape
        n = h * w
        xf = x.reshape(b, c, n)
        q = jnp.einsum('bcn,oc->bon', xf, Wq) + bq[None, :, None]
        k = jnp.einsum('bcn,oc->bon', xf, Wk) + bk[None, :, None]
        v = jnp.einsum('bcn,oc->bon', xf, Wv) + bv[None, :, None]
        energy = jnp.einsum('bhi,bhj->bij', q, k)
        weight = jax.nn.softmax(energy, axis=-1)
        attn = jnp.einsum('bcj,bij->bci', v, weight)
        return x + attn.reshape(b, c, h, w)

    def _L1_conv_ref(x, Wf, bf, Wg, bg, Wh, bh, gamma):
        import jax, jax.numpy as jnp
        import numpy as np
        B, C, W, H = x.shape
        N = W * H
        xf = x.reshape(B, C, N)
        f = jnp.einsum('kc,bcn->bkn', Wf, xf) + bf[None, :, None]
        g = jnp.einsum('kc,bcn->bkn', Wg, xf) + bg[None, :, None]
        h = jnp.einsum('oc,bcn->bon', Wh, xf) + bh[None, :, None]
        attn = jax.nn.softmax(jnp.einsum('bki,bkj->bij', f, g), axis=-1)
        sa = jnp.einsum('bcj,bji->bci', h, attn).reshape(B, C, W, H)
        return gamma[0] * sa + x

    def _L2_conv_ref(x, Wq, Wk, Wv, gamma):
        import jax, jax.numpy as jnp
        import numpy as np
        B, C, H, W = x.shape
        N = H * W
        xt = x.reshape(B, C, N)
        q = jnp.einsum('oc,bcn->bon', Wq, xt)
        k = jnp.einsum('oc,bcn->bon', Wk, xt)
        v = jnp.einsum('oc,bcn->bon', Wv, xt)
        energy = jnp.einsum('bon,bom->bnm', q, k)
        attn = jax.nn.softmax(energy, axis=-1)
        out = jnp.einsum('bcm,bnm->bcn', v, attn).reshape(B, C, H, W)
        return gamma * out + x

    def _L3_conv_ref(x, gn_w, gn_b, qkv_w, qkv_b, proj_w, proj_b, gproj_w, gproj_b):
        import jax, jax.numpy as jnp
        import numpy as np
        CHANNELS = 64
        HEADS = 8
        GROUPS = 32
        EPS = 1e-05
        b, c, h, w = x.shape
        n = h * w
        hd = c // HEADS
        scale = hd ** (-0.5)
        xg = x.reshape(b, GROUPS, -1)
        mu = jnp.mean(xg, axis=-1, keepdims=True)
        var = jnp.mean((xg - mu) ** 2, axis=-1, keepdims=True)
        xn = ((xg - mu) * jax.lax.rsqrt(var + EPS)).reshape(b, c, h, w)
        xn = xn * gn_w[None, :, None, None] + gn_b[None, :, None, None]
        gfeat = jnp.mean(xn, axis=(2, 3))
        gfeat = gfeat @ gproj_w.T + gproj_b
        qkv = jnp.einsum('bchw,oc->bohw', xn, qkv_w) + qkv_b[None, :, None, None]
        q, k, v = (qkv[:, :c], qkv[:, c:2 * c], qkv[:, 2 * c:])
        q = q.reshape(b, HEADS, hd, n).transpose(0, 1, 3, 2)
        k = k.reshape(b, HEADS, hd, n) + gfeat.reshape(b, HEADS, hd, 1) * 0.1
        v = v.reshape(b, HEADS, hd, n).transpose(0, 1, 3, 2)
        attn = jax.nn.softmax(jnp.einsum('bhnd,bhdm->bhnm', q, k) * scale, axis=-1)
        out = jnp.einsum('bhnm,bhmd->bhnd', attn, v)
        out = out.transpose(0, 1, 3, 2).reshape(b, c, h, w)
        out = jnp.einsum('bchw,oc->bohw', out, proj_w) + proj_b[None, :, None, None]
        out = out + gfeat[:, :, None, None] * 0.1
        return out + x

    def _gn(v, G=32, eps=1e-05):
        B_, C_, H_, W_ = v.shape
        g = v.reshape(B_, G, C_ // G, H_, W_)
        m = jnp.mean(g, axis=(2, 3, 4), keepdims=True)
        s = jnp.var(g, axis=(2, 3, 4), keepdims=True)
        return ((g - m) / jnp.sqrt(s + eps)).reshape(v.shape)

    def _ln_c(v, eps=1e-06):
        m = jnp.mean(v, axis=1, keepdims=True)
        s = jnp.var(v, axis=1, keepdims=True)
        return (v - m) / jnp.sqrt(s + eps)

    def _ln_t(v, eps=1e-05):
        m = jnp.mean(v, axis=-1, keepdims=True)
        s = jnp.var(v, axis=-1, keepdims=True)
        return (v - m) / jnp.sqrt(s + eps)

    def _to_tokens(v):
        B_, C_, H_, W_ = v.shape
        return v.reshape(B_, C_, H_ * W_).transpose(0, 2, 1)

    def _from_tokens(t, like):
        B_, C_, H_, W_ = like.shape
        return t.transpose(0, 2, 1).reshape(B_, C_, H_, W_)
    x = _L0_conv_ref(x, L0_conv_Wq, L0_conv_bq, L0_conv_Wk, L0_conv_bk, L0_conv_Wv, L0_conv_bv)
    x = _L1_conv_ref(x, L1_conv_Wf, L1_conv_bf, L1_conv_Wg, L1_conv_bg, L1_conv_Wh, L1_conv_bh, L1_conv_gamma)
    x = _L2_conv_ref(x, L2_conv_Wq, L2_conv_Wk, L2_conv_Wv, L2_conv_gamma)
    x = _L3_conv_ref(x, L3_conv_gn_w, L3_conv_gn_b, L3_conv_qkv_w, L3_conv_qkv_b, L3_conv_proj_w, L3_conv_proj_b, L3_conv_gproj_w, L3_conv_gproj_b)
    return x

_drawn_inputs = setup_inputs


def setup_inputs(seed=0):
    import zlib

    import numpy as np

    out = dict(_drawn_inputs(seed))
    spreads = {'L1_conv_bf': (0.0, 0.614),
     'L1_conv_bg': (0.0, 0.8),
     'L1_conv_bh': (0.0, 0.367),
     'L3_conv_gn_w': (1.0, 0.2),
     'L3_conv_gn_b': (0.0, 0.1),
     'L3_conv_qkv_b': (0.0, 0.1),
     'L3_conv_proj_b': (0.0, 0.1),
     'L3_conv_gproj_b': (0.0, 0.8)}
    factors = {'L0_conv_Wq': 8.0,
     'L0_conv_bq': 8.0,
     'L0_conv_Wk': 8.0,
     'L0_conv_bk': 8.0,
     'L0_conv_Wv': 3.95,
     'L3_conv_gproj_w': 5.68}
    for name, (base, spread) in spreads.items():
        noise = np.random.default_rng([zlib.crc32(name.encode()), seed]).standard_normal(out[name].shape)
        drawn = base * np.exp(spread * noise) if base else spread * noise
        out[name] = jnp.asarray(drawn.astype(out[name].dtype))
    for name, factor in factors.items():
        out[name] = (out[name] * factor).astype(out[name].dtype)
    return out
```

```python
from contextlib import ExitStack

import numpy as np
import concourse.bass as bass
from concourse import mybir

B, C, N = 4, 64, 256
PAIRS = 2
P = 128
HALF = N // 2
HID0 = 32
HID1 = 8
HEADS, HD = 8, 8
GROUP = 2
KINDS1 = 4
KINDS3 = 3
Q_LOW = (2, 3)
K_LOW = (1, 3)
QUAD = 32
MAXROW = KINDS3 * HD
HPG = P // QUAD
EPS = 1e-5

GROUPS = [
    [("wq0", P), ("wk0", P), ("wv0", P), ("vb0", P), ("cols", 16)],
    [("ident", P), ("w1", P), ("wv1", P), ("vb1", P)],
    [("wq2", P), ("wk2", P), ("wv2", P), ("fold", C), ("gavg", P)],
    [("wq3", P), ("wk3", P), ("wv3", P), ("vb3", P), ("wg3", P), ("wp3", P)],
]
COLS = ["bq0", "bk0", "b1", "low1", "gamma1", "gamma2", "bq3", "bk3", "ones_rows", "keep_rows",
        "gn_w", "gn_b", "proj_b", "gproj_b"]


def places():
    at, where, spans = 0, {}, []
    for group in GROUPS:
        first = at
        for name, width in group:
            where[name] = (at, width)
            at += width
        spans.append((first, at))
    return where, spans, at


def l3_bank_a_items():
    order = [("proj", 0)]
    for s in range(4):
        order += [("score", s, j) for j in range(HPG)]
        if s < 3:
            order.append(("proj", s + 1))
        order.append(("aug", s))
        if s == 2:
            order.append(("turn", 0))
    order += [("turn", 1), ("back",), ("out",)]
    return order


def conv_attention_chain(nc: bass.Bass, x: bass.AP, pack: bass.AP, out: bass.AP):
    f32, f32r = mybir.dt.float32, mybir.dt.float32r
    ALU, ACT, AX = mybir.AluOpType, mybir.ActivationFunctionType, mybir.AxisListType
    where, spans, width = places()
    x_pairs = x.rearrange("(p b) c h w -> p (b c) (h w)", p=PAIRS)
    out_pairs = out.rearrange("(p b) c h w -> p (b c) (h w)", p=PAIRS)
    A_ORDER = l3_bank_a_items()
    A_ITEM = {item: n for n, item in enumerate(A_ORDER)}
    R = range(PAIRS)

    with ExitStack() as ctx:
        def sb(name, shape, dt=f32):
            return ctx.enter_context(nc.sbuf_tensor(name, shape, dt))

        def pair_sb(name, shape, dt=f32):
            return [sb(f"{name}{p}", shape, dt) for p in R]

        def pair_sem(name):
            return [ctx.enter_context(nc.semaphore(f"{name}{p}")) for p in R]

        W = sb("W", [P, width])

        def w(name):
            a, n = where[name]
            return W[:, a:a + n]

        def col(name):
            a = where["cols"][0] + COLS.index(name)
            return W[:, a:a + 1]

        ident = w("ident")
        ident_r = sb("ident_r", [P, P], f32r)
        low_bias1 = sb("low_bias1", [P, 1])
        X = pair_sb("X", [P, N])
        Qs = pair_sb("Q", [P, N])
        Ks = pair_sb("K", [P, N])
        V = pair_sb("V", [P, 2, P])
        VS = pair_sb("VS", [P, 2, P])
        M1 = pair_sb("M1", [P, N], f32r)
        F1 = pair_sb("F1", [C, N], f32r)
        G1 = pair_sb("G1", [C, N], f32r)
        NM = [[sb(f"NM{p}{b}", [P, 2]) for b in range(2)] for p in R]
        SUM = [[sb(f"SUM{p}{b}", [P, 2]) for b in range(2)] for p in R]
        RS = [[sb(f"RS{p}{b}", [P, 2]) for b in range(2)] for p in R]
        E = [[sb(f"E{p}{b}", [P, 2, N]) for b in range(2)] for p in R]
        ET = [[sb(f"ET{p}{b}", [P, 2, N]) for b in range(2)] for p in R]
        ST6 = pair_sb("ST6", [P, 6])
        MV = pair_sb("MV", [P, 2])
        GM = pair_sb("GM", [P, 8])
        half_pow = sb("half_pow", [P, 1])
        XN = pair_sb("XN", [P, N])
        QH, QL = pair_sb("QH", [P, N], f32r), pair_sb("QL", [P, N], f32r)
        KH, KL = pair_sb("KH", [P, N], f32r), pair_sb("KL", [P, N], f32r)
        sel = {k: sb(f"sel_{k}", [P, HEADS, QUAD], f32r) for k in ("qh", "ql", "kh", "kl")}
        QKS = [[sb(f"QKS{p}{i}", [P, 2, N], f32r) for i in range(2)] for p in R]
        QSA = pair_sb("QSA", [P, N], f32r)
        NM3 = pair_sb("NM3", [P, 2, HPG])
        AUGW = pair_sb("AUGW", [P, 2, P], f32r)
        E3 = [[[sb(f"E3{p}{i}{t}", [P, 2, 2, N]) for t in range(2)] for i in range(2)] for p in R]
        VA = [[sb(f"VA{p}{b}", [P, 2, HEADS, QUAD]) for b in range(2)] for p in R]
        OS = pair_sb("OS", [P, 2, N])
        R3 = pair_sb("R3", [P, 4, HPG])
        ON = pair_sb("ON", [P, 2, 2, C])
        OT = pair_sb("OT", [P, N])
        Y = pair_sb("Y", [P, N])

        PS = [ctx.enter_context(nc.psum_tensor(f"PS{p}", [P, 2048], f32)) for p in R]
        bank_a = [PS[p][:, 0:512] for p in R]
        bank_b = [PS[p][:, 512:1024] for p in R]
        bank_c = [PS[p][:, 1024:1536] for p in R]
        bank_d = [PS[p][:, 1536:2048] for p in R]
        bank_bc = [PS[p][:, 512:1536] for p in R]

        x_loaded = pair_sem("x_loaded")
        w_loaded = [ctx.enter_context(nc.semaphore(f"w_loaded{g}")) for g in range(len(GROUPS))]
        prep_vector = ctx.enter_context(nc.semaphore("prep_vector"))
        prep_pool = ctx.enter_context(nc.semaphore("prep_pool"))
        q_made, k_made, v_made = pair_sem("q_made"), pair_sem("k_made"), pair_sem("v_made")
        q_out, k_out, v_out = pair_sem("q_out"), pair_sem("k_out"), pair_sem("v_out")
        high_out = pair_sem("high_out")
        scores = pair_sem("scores")
        maxima = pair_sem("maxima")
        exps = pair_sem("exps")
        recips = pair_sem("recips")
        divided = pair_sem("divided")
        turned = pair_sem("turned")
        turned_out = pair_sem("turned_out")
        turned_out1 = pair_sem("turned_out1")
        mixed = pair_sem("mixed")
        x_new = pair_sem("x_new")
        stat = pair_sem("stat")
        group_mean, rstd, xn_out, gfeat_made = (pair_sem(n) for n in
                                                ("group_mean", "rstd", "xn_out", "gfeat_made"))
        q_high, q_low, k_high, k_low = (pair_sem(n) for n in ("q_high", "q_low", "k_high", "k_low"))
        a_full = pair_sem("a_full")
        maxima3, max_high = pair_sem("maxima3"), pair_sem("max_high")
        max_parts, aug_out = pair_sem("max_parts"), pair_sem("aug_out")
        stack_out = pair_sem("stack_out")
        scores3, exps3, mixed3 = pair_sem("scores3"), pair_sem("exps3"), pair_sem("mixed3")
        o_out, recips3, on_out, ot_out = (pair_sem(n) for n in ("o_out", "recips3", "on_out", "ot_out"))
        y_out, stored = pair_sem("y_out"), pair_sem("stored")

        block = ctx.enter_context(nc.Block())

        @block.sync
        def _(sp):
            sp.dma_start(X[0][:, :], x_pairs[0]).then_inc(x_loaded[0], 16)
            for g, (a, z) in enumerate(spans):
                sp.dma_start(W[:, a:z], pack[:, a:z]).then_inc(w_loaded[g], 16)
                if g == 0:
                    sp.dma_start(X[1][:, :], x_pairs[1]).then_inc(x_loaded[1], 16)
            for p in R:
                sp.wait_ge(y_out[p], 1)
                sp.dma_start(out_pairs[p], Y[p][:, :]).then_inc(stored[p], 16)
            for p in R:
                sp.wait_ge(stored[p], 16)

        @block.gpsimd
        def _(pool):
            for p in R:
                pool.memset(AUGW[p][:, :, :].bitcast(f32), 0.0).then_inc(prep_pool, 1)
                for b in range(2):
                    pool.memset(VA[p][b][:, :, :, :], 0.0).then_inc(prep_pool, 1)
            for k in sel:
                pool.memset(sel[k][:, :, :].bitcast(f32), 0.0).then_inc(prep_pool, 1)
            pool.memset(half_pow[:, :], -0.5).then_inc(prep_pool, 1)
            zeroed = 3 * PAIRS + len(sel) + 1
            pool.wait_ge(prep_pool, zeroed)
            for p in R:
                for b in range(2):
                    pool.memset(VA[p][b][:, :, :, HD:HD + 1], 1.0).then_inc(prep_pool, 1)
            pool.wait_ge(w_loaded[1], 16)
            pool.wait_ge(w_loaded[2], 16)
            pool.tensor_copy(ident_r[:, :], ident).then_inc(prep_pool, 1)
            fold = w("fold").rearrange("p (h d) -> p h d", d=HD)
            for side, low in (("q", Q_LOW), ("k", K_LOW)):
                for kind in range(KINDS3):
                    part = side + ("l" if kind in low else "h")
                    pool.tensor_copy(sel[part][:, :, kind * HD:(kind + 1) * HD], fold)\
                        .then_inc(prep_pool, 1)
            for p in R:
                pool.wait_ge(stat[p], 5)
                pool.tensor_tensor(GM[p][:, 3:4], GM[p][:, 2:3], half_pow[:, :], ALU.pow)\
                    .then_inc(rstd[p], 1)
        PREPARED = 3 * PAIRS + 4 + 1 + 2 * PAIRS + 1 + 2 * KINDS3

        @block.tensor
        def _(pe):
            def halves(t, rows, half):
                return t[rows, half * HALF:(half + 1) * HALF]

            def values(p, lhs, weights):
                for half in range(2):
                    mm = pe.matmul(bank_c[p][:, half * P:(half + 1) * P],
                                   lhs[:, half * HALF:(half + 1) * HALF], weights,
                                   start=True, stop=True)
                mm.then_inc(v_made[p], 1)

            def project(layer, p):
                if layer == 0:
                    pe.wait_ge(x_loaded[p], 16)
                    if p == 0:
                        pe.wait_ge(w_loaded[0], 16)
                else:
                    if p == 0:
                        pe.wait_ge(w_loaded[layer], 16)
                    pe.wait_ge(x_new[p], layer)
                if layer == 1:
                    pe.matmul(bank_a[p][:, 0:N], w("w1"), X[p][:, :], start=True, stop=True)\
                        .then_inc(q_made[p], 1)
                    values(p, X[p], w("wv1"))
                    return
                pe.matmul(bank_a[p][:, 0:N], w(f"wq{layer}"), X[p][:, :], start=True, stop=True)\
                    .then_inc(q_made[p], 1)
                pe.matmul(bank_b[p][:, 0:N], w(f"wk{layer}"), X[p][:, :], start=True, stop=True)\
                    .then_inc(k_made[p], 1)
                values(p, X[p], w(f"wv{layer}"))

            def score(layer, p):
                pe.wait_ge(q_out[p], layer + 1)
                pe.wait_ge(k_out[p], layer + 1)
                lhs, rhs = (F1[p], G1[p]) if layer == 1 else (Qs[p], Ks[p])
                k = QUAD if layer == 1 else C
                for b, bank in enumerate((bank_a[p], bank_b[p])):
                    rows = slice(b * k, b * k + k)
                    for half in range(2):
                        mm = pe.matmul(bank[:, half * N:(half + 1) * N], halves(lhs, rows, half),
                                       rhs[rows, :], start=True, stop=True)
                    mm.then_inc(scores[p], 1)

            def turn(layer, p):
                for b, bank in enumerate((bank_a[p], bank_b[p])):
                    pe.wait_ge(divided[p], 2 * layer + b + 1)
                    if layer == 0 and p == 0 and b == 0:
                        pe.wait_ge(w_loaded[1], 16)
                    for m in range(2):
                        for n in range(2):
                            tp = pe.transpose(bank[:, m * N + n * HALF:m * N + (n + 1) * HALF],
                                              E[p][b][:, n, m * HALF:(m + 1) * HALF], ident)
                    tp.then_inc(turned[p], 1)

            def mix(layer, p):
                pe.wait_ge(v_out[p], layer + 1)
                if layer == 1:
                    pe.wait_ge(divided[p], 4)
                else:
                    pe.wait_ge(turned_out[p], layer // 2 + 1)
                    pe.wait_ge(turned_out1[p], layer // 2 + 1)
                lhs, rhs = (VS[p], E[p]) if layer == 1 else (V[p], ET[p])
                for m in range(2):
                    for b in range(2):
                        mm = pe.matmul(bank_c[p][b * C:(b + 1) * C, 0:N],
                                       lhs[:, m, b * C:(b + 1) * C], rhs[b][:, m, :],
                                       start=(m == 0), stop=(m == 1))
                mm.then_inc(mixed[p], 1)

            for layer in range(3):
                project(layer, 0)
                if layer > 0:
                    mix(layer - 1, 1)
                score(layer, 0)
                project(layer, 1)
                if layer != 1:
                    turn(layer, 0)
                score(layer, 1)
                mix(layer, 0)
                if layer != 1:
                    turn(layer, 1)

            def group_means(p):
                pe.wait_ge(stat[p], 2)
                pe.matmul(bank_d[p][:, 0:2], w("gavg"), MV[p][:, :], start=True, stop=True)\
                    .then_inc(group_mean[p], 1)

            def project3(p):
                if p == 0:
                    pe.wait_ge(w_loaded[3], 16)
                pe.wait_ge(xn_out[p], 1)
                pe.matmul(bank_d[p][:, 0:1], w("wg3"), GM[p][:, 6:7], start=True, stop=True)\
                    .then_inc(gfeat_made[p], 1)
                pe.matmul(bank_a[p][:, 0:N], w("wq3"), XN[p][:, :], start=True, stop=True)\
                    .then_inc(q_made[p], 1)
                pe.matmul(bank_b[p][:, 0:N], w("wk3"), XN[p][:, :], start=True, stop=True)\
                    .then_inc(k_made[p], 1)
                values(p, XN[p], w("wv3"))

            def a_turn(p, item):
                if A_ITEM[item] > 0:
                    name, *at = A_ORDER[A_ITEM[item] - 1]
                    if name == "proj":
                        pe.wait_ge(stack_out[p], at[0] + 1)
                    elif name == "score":
                        pe.wait_ge(maxima3[p], 4 * at[0] + at[1] + 1)
                    elif name == "aug":
                        pe.wait_ge(aug_out[p], at[0] + 1)
                    elif name == "turn":
                        pe.wait_ge(on_out[p], at[0] + 1)
                    else:
                        pe.wait_ge(ot_out[p], 1)

            def stacks(s, p):
                b, g = divmod(s, 2)
                rows = slice(b * C, (b + 1) * C)
                a_turn(p, ("proj", s))
                if s == 0:
                    pe.wait_ge(prep_pool, PREPARED)
                    pe.wait_ge(q_low[p], 1)
                    pe.wait_ge(q_high[p], 1)
                    pe.wait_ge(k_high[p], 1)
                    pe.wait_ge(k_low[p], 1)
                for i, (side, hi, lo) in enumerate((("q", QH, QL), ("k", KH, KL))):
                    for part, t in (("h", hi), ("l", lo)):
                        lhs = sel[side + part][rows, g * HPG:(g + 1) * HPG, :]
                        mm = pe.matmul(bank_a[p][:, i * N:(i + 1) * N],
                                       lhs.rearrange("c h r -> c (h r)"), t[p][rows, :],
                                       start=(part == "h"), stop=(part == "l"))
                mm.then_inc(a_full[p], 1)

            def score3(s, j, p):
                a_turn(p, ("score", s, j))
                pe.wait_ge(stack_out[p], s + 1)
                t = QKS[p][s % 2]
                rows = slice(j * QUAD, j * QUAD + MAXROW)
                for half in range(2):
                    mm = pe.matmul(bank_a[p][:, half * N:(half + 1) * N],
                                   t[rows, 0, half * HALF:(half + 1) * HALF], t[rows, 1, :],
                                   start=True, stop=True)
                mm.then_inc(a_full[p], 1)

            def max_rows(s, p):
                a_turn(p, ("aug", s))
                pe.wait_ge(max_parts[p], s + 1)
                for half in range(2):
                    mm = pe.matmul(bank_a[p][:, half * HALF:(half + 1) * HALF],
                                   AUGW[p][:, half, :], ident_r[:, :], start=True, stop=True)
                mm.then_inc(a_full[p], 1)

            def score_t(s, two, p):
                i = 2 * s + two
                if i == 0:
                    pe.wait_ge(v_out[p], 4)
                else:
                    pe.wait_ge(exps3[p], i)
                if two == 0:
                    pe.wait_ge(aug_out[p], s + 1)
                for m in range(2):
                    for i in range(2):
                        j = 2 * two + i
                        rows = slice(j * QUAD, (j + 1) * QUAD)
                        to = (2 * i + m) * N
                        mm = pe.matmul(bank_bc[p][:, to:to + N],
                                       QKS[p][s % 2][rows, 1, m * HALF:(m + 1) * HALF],
                                       QSA[p][rows, :], start=True, stop=True)
                mm.then_inc(scores3[p], 1)

            def mix3(s, p):
                b, g = divmod(s, 2)
                pe.wait_ge(exps3[p], 2 * s + 2)
                if s == 2:
                    pe.wait_ge(o_out[p], 1)
                for m in range(2):
                    for j in range(HPG):
                        e = E3[p][s % 2][j // 2][:, j % 2, m, :]
                        mm = pe.matmul(bank_d[p][j * QUAD:(j + 1) * QUAD, g * N:(g + 1) * N],
                                       VA[p][b][:, m, g * HPG + j, :], e,
                                       start=(m == 0), stop=(m == 1))
                mm.then_inc(mixed3[p], 1)

            def turn3(b, p):
                a_turn(p, ("turn", b))
                pe.wait_ge(o_out[p], b + 1)
                for half in range(2):
                    for g in range(2):
                        i = 2 * half + g
                        tp = pe.transpose(bank_a[p][:, i * P:(i + 1) * P],
                                          OS[p][:, g, half * HALF:(half + 1) * HALF], ident)
                tp.then_inc(a_full[p], 1)

            def back3(p):
                a_turn(p, ("back",))
                pe.wait_ge(on_out[p], 2)
                for half in range(2):
                    tp = pe.transpose(bank_a[p][:, half * HALF:(half + 1) * HALF],
                                      ON[p][:, half, :, :].rearrange("q b c -> q (b c)"), ident)
                tp.then_inc(a_full[p], 1)

            def out3(p):
                a_turn(p, ("out",))
                pe.wait_ge(ot_out[p], 1)
                pe.matmul(bank_a[p][:, 0:N], w("wp3"), OT[p][:, :], start=True, stop=True)\
                    .then_inc(a_full[p], 1)

            group_means(0)
            mix(2, 1)
            project3(0)
            group_means(1)
            stacks(0, 0)
            project3(1)
            stacks(0, 1)
            for s in range(5):
                now, before = s < 4, s > 0
                for p in R:
                    if now:
                        score3(s, 0, p)
                    if before:
                        score_t(s - 1, 0, p)
                for p in R:
                    if now:
                        score3(s, 1, p)
                    if before:
                        score_t(s - 1, 1, p)
                for j in (2, 3):
                    for p in R:
                        if now:
                            score3(s, j, p)
                        if before and j == 3:
                            mix3(s - 1, p)
                for p in R:
                    if s < 3:
                        stacks(s + 1, p)
                    if now:
                        max_rows(s, p)
                if s == 2:
                    for p in R:
                        turn3(0, p)
            for step in (lambda p: turn3(1, p), back3, out3):
                for p in R:
                    step(p)

        @block.scalar
        def _(act):
            def queries(layer, p):
                if layer == 0 and p == 0:
                    act.wait_ge(prep_vector, 1)
                act.wait_ge(q_made[p], layer + 1)
                if layer == 0:
                    act.activation(Qs[p][:, :], bank_a[p][:, 0:N], ACT.Identity, bias=col("bq0"))\
                        .then_inc(q_out[p], 1)
                elif layer == 1:
                    act.activation(M1[p][:, :], bank_a[p][:, 0:N], ACT.Identity,
                                   bias=low_bias1[:, :], scale=col("low1")).then_inc(high_out[p], 1)
                else:
                    act.activation(Qs[p][:, :], bank_a[p][:, 0:N], ACT.Copy).then_inc(q_out[p], 1)
                    act.wait_ge(v_made[p], 3)
                    act.activation(V[p][:, :, :].rearrange("t h c -> t (h c)"), bank_c[p][:, 0:N],
                                   ACT.Copy).then_inc(v_out[p], 1)

            def exponents(layer, p):
                for b, bank in enumerate((bank_a[p], bank_b[p])):
                    act.wait_ge(maxima[p], 2 * layer + b + 1)
                    for half in range(2):
                        e = act.activation(E[p][b][:, half, :], bank[:, half * N:(half + 1) * N],
                                           ACT.Exp, bias=NM[p][b][:, half:half + 1],
                                           accum_out=SUM[p][b][:, half:half + 1])
                    e.then_inc(exps[p], 1)

            def turned_copy(layer, p):
                act.wait_ge(turned[p], 2 * (layer // 2) + 1)
                act.activation(ET[p][0][:, :, :].rearrange("m h n -> m (h n)"), bank_a[p][:, :],
                               ACT.Copy).then_inc(turned_out[p], 1)

            for layer in range(3):
                queries(layer, 0)
                exponents(layer, 0)
                queries(layer, 1)
                if layer != 1:
                    turned_copy(layer, 0)
                exponents(layer, 1)
                if layer != 1:
                    turned_copy(layer, 1)

            def high_parts(p):
                act.wait_ge(q_made[p], 4)
                act.activation(QH[p][:, :], bank_a[p][:, 0:N], ACT.Identity, bias=col("bq3"))\
                    .then_inc(q_high[p], 1)
                act.wait_ge(k_made[p], 3)
                act.wait_ge(stat[p], 11)
                act.activation(KH[p][:, :], bank_b[p][:, 0:N], ACT.Identity, bias=GM[p][:, 2:3])\
                    .then_inc(k_high[p], 1)

            def stack_copy(s, p):
                act.wait_ge(a_full[p], A_ITEM[("proj", s)] + 1)
                if s >= 2:
                    act.wait_ge(scores3[p], 2 * (s - 2) + 2)
                act.activation(QKS[p][s % 2][:, :, :].rearrange("r i n -> r (i n)"), bank_a[p][:, :],
                               ACT.Identity, bias=col("ones_rows"))\
                    .then_inc(stack_out[p], 1)

            def exps_t(s, two, p):
                act.wait_ge(scores3[p], 2 * s + two + 1)
                if s >= 2:
                    act.wait_ge(mixed3[p], s - 1)
                act.activation(E3[p][s % 2][two][:, :, :, :].rearrange("k j m q -> k (j m q)"),
                               bank_bc[p][:, :], ACT.Exp, scale=float(HD) ** -0.5)\
                    .then_inc(exps3[p], 1)

            def o_copy(b, p):
                act.wait_ge(mixed3[p], 2 * (b + 1))
                act.activation(OS[p][:, :, :].rearrange("r g n -> r (g n)"), bank_d[p][:, :],
                               ACT.Copy).then_inc(o_out[p], 1)

            for p in R:
                high_parts(p)
                stack_copy(0, p)
            for s in range(5):
                if s > 0:
                    for two in range(2):
                        for p in R:
                            exps_t(s - 1, two, p)
                if s in (2, 4):
                    for p in R:
                        o_copy(s // 2 - 1, p)
                if s < 3:
                    for p in R:
                        stack_copy(s + 1, p)
            for p in R:
                act.wait_ge(a_full[p], A_ITEM[("back",)] + 1)
                act.activation(OT[p][:, :], bank_a[p][:, 0:N], ACT.Copy).then_inc(ot_out[p], 1)

        @block.vector
        def _(dve):
            dve.wait_ge(w_loaded[0], 16)
            dve.tensor_tensor(low_bias1[:, :], col("b1"), col("low1"), ALU.mult)\
                .then_inc(prep_vector, 1)

            def keys_and_values(layer, p):
                if layer == 1:
                    dve.wait_ge(high_out[p], 1)
                    for dst, rows, done in ((F1, slice(0, C), q_out), (G1, slice(C, P), k_out)):
                        dve.scalar_tensor_tensor(dst[p][:, :], bank_a[p][rows, 0:N],
                                                 col("b1")[rows, :], M1[p][rows, :].bitcast(f32),
                                                 ALU.add, ALU.subtract).then_inc(done[p], 1)
                else:
                    dve.wait_ge(k_made[p], layer // 2 + 1)
                    if layer == 0:
                        dve.tensor_scalar(Ks[p][:, :], bank_b[p][:, 0:N], col("bk0"), None, ALU.add)\
                            .then_inc(k_out[p], 1)
                    else:
                        dve.tensor_copy(Ks[p][:, :], bank_b[p][:, 0:N]).then_inc(k_out[p], 1)
                if layer < 2:
                    dve.wait_ge(v_made[p], layer + 1)
                    bias = w(f"vb{layer}").unsqueeze(1).broadcast_to([P, 2, P])
                    dve.tensor_tensor(V[p][:, :, :], bank_c[p][:, 0:N].rearrange(
                        "t (h c) -> t h c", h=2), bias, ALU.add).then_inc(v_out[p], 1)

            def row_maxima(layer, p):
                for b, bank in enumerate((bank_a[p], bank_b[p])):
                    i = 2 * layer + b
                    dve.wait_ge(scores[p], i + 1)
                    dve.tensor_reduce(NM[p][b][:, :], bank.rearrange("r (h c) -> r h c", h=2), AX.X,
                                      ALU.max, negate=True).then_inc(maxima[p], 1)

            def divide(layer, p):
                for b in range(2):
                    i = 2 * layer + b
                    dve.wait_ge(exps[p], i + 1)
                    dve.reciprocal(RS[p][b][:, :], SUM[p][b][:, :]).then_inc(recips[p], 1)
                    dve.wait_ge(recips[p], i + 1)
                    if layer == 1:
                        cols = slice(b * C, (b + 1) * C)
                        dve.wait_ge(v_out[p], 2)
                        dve.tensor_tensor(VS[p][:, :, cols], V[p][:, :, cols],
                                          RS[p][b][:, :].unsqueeze(2).broadcast_to([P, 2, C]),
                                          ALU.mult).then_inc(divided[p], 1)
                    else:
                        for half in range(2):
                            d = dve.tensor_scalar(E[p][b][:, half, :], E[p][b][:, half, :],
                                                  RS[p][b][:, half:half + 1], None, ALU.mult)
                        d.then_inc(divided[p], 1)

            def turned_copy(layer, p):
                dve.wait_ge(turned[p], 2 * (layer // 2) + 2)
                dve.tensor_copy(ET[p][1][:, :, :].rearrange("m h n -> m (h n)"), bank_b[p][:, :])\
                    .then_inc(turned_out1[p], 1)

            def residual(layer, p):
                dve.wait_ge(mixed[p], layer + 1)
                if layer == 0:
                    dve.tensor_tensor(X[p][:, :], bank_c[p][:, 0:N], X[p][:, :], ALU.add)\
                        .then_inc(x_new[p], 1)
                else:
                    dve.scalar_tensor_tensor(X[p][:, :], bank_c[p][:, 0:N], col(f"gamma{layer}"),
                                             X[p][:, :], ALU.mult, ALU.add).then_inc(x_new[p], 1)

            for layer in range(3):
                keys_and_values(layer, 0)
                if layer > 0:
                    residual(layer - 1, 1)
                row_maxima(layer, 0)
                divide(layer, 0)
                keys_and_values(layer, 1)
                row_maxima(layer, 1)
                if layer != 1:
                    turned_copy(layer, 0)
                residual(layer, 0)
                divide(layer, 1)
                if layer != 1:
                    turned_copy(layer, 1)

            def small(p, n, ins):
                ins.then_inc(stat[p], 1)
                dve.wait_ge(stat[p], n)

            def statistics(p):
                dve.wait_ge(x_new[p], 3)
                small(p, 1, dve.bn_stats(ST6[p][:, :], X[p][:, :]))
                small(p, 2, dve.bn_aggr(MV[p][:, :], ST6[p][:, :]))

            def normalise(p):
                m = GM[p]
                dve.wait_ge(group_mean[p], 1)
                small(p, 3, dve.tensor_tensor(m[:, 0:1], bank_d[p][:, 0:1], MV[p][:, 0:1],
                                              ALU.subtract))
                small(p, 4, dve.tensor_tensor(m[:, 1:2], m[:, 0:1], m[:, 0:1], ALU.mult))
                small(p, 5, dve.scalar_tensor_tensor(m[:, 2:3], bank_d[p][:, 1:2], EPS, m[:, 1:2],
                                                     ALU.add, ALU.add))
                dve.wait_ge(rstd[p], 1)
                small(p, 6, dve.tensor_tensor(m[:, 4:5], m[:, 3:4], col("gn_w"), ALU.mult))
                small(p, 7, dve.tensor_tensor(m[:, 7:8], bank_d[p][:, 0:1], m[:, 4:5], ALU.mult))
                small(p, 8, dve.tensor_tensor(m[:, 5:6], col("gn_b"), m[:, 7:8], ALU.subtract))
                small(p, 9, dve.scalar_tensor_tensor(m[:, 6:7], MV[p][:, 0:1], m[:, 4:5],
                                                     m[:, 5:6], ALU.mult, ALU.add))
                dve.tensor_scalar(XN[p][:, :], X[p][:, :], m[:, 4:5], m[:, 5:6], ALU.mult, ALU.add)\
                    .then_inc(xn_out[p], 1)

            def global_feature(p):
                m = GM[p]
                dve.wait_ge(gfeat_made[p], 1)
                small(p, 10, dve.tensor_scalar(m[:, 0:1], bank_d[p][:, 0:1], col("gproj_b"), 0.1,
                                               ALU.add, ALU.mult))
                small(p, 11, dve.tensor_tensor(m[:, 2:3], m[:, 0:1], col("bk3"), ALU.add))
                small(p, 12, dve.tensor_tensor(m[:, 1:2], m[:, 0:1], col("proj_b"), ALU.add))

            def low_parts(p):
                dve.wait_ge(q_high[p], 1)
                dve.scalar_tensor_tensor(QL[p][:, :], bank_a[p][:, 0:N], col("bq3"),
                                         QH[p][:, :].bitcast(f32), ALU.add, ALU.subtract)\
                    .then_inc(q_low[p], 1)
                dve.wait_ge(k_high[p], 1)
                dve.scalar_tensor_tensor(KL[p][:, :], bank_b[p][:, 0:N], GM[p][:, 2:3],
                                         KH[p][:, :].bitcast(f32), ALU.add, ALU.subtract)\
                    .then_inc(k_low[p], 1)

            def values3(p):
                dve.wait_ge(v_made[p], 4)
                if p == 0:
                    dve.wait_ge(prep_pool, PREPARED)
                for b in range(2):
                    src = bank_c[p][:, 0:N].rearrange("t (h b e d) -> t h b e d", h=2, b=2, d=HD)
                    bias = w("vb3")[:, 0:C].rearrange("t (e d) -> t e d", d=HD)
                    v = dve.tensor_tensor(VA[p][b][:, :, :, 0:HD], src[:, :, b],
                                          bias.unsqueeze(1).broadcast_to([P, 2, HEADS, HD]), ALU.add)
                v.then_inc(v_out[p], 1)

            def maxima_of(s, j, p):
                dve.wait_ge(a_full[p], A_ITEM[("score", s, j)] + 1)
                dve.tensor_reduce(NM3[p][:, :, j], bank_a[p].rearrange("q (h k) -> q h k", h=2),
                                  AX.X, ALU.max, negate=True).then_inc(maxima3[p], 1)

            def parts_of_maxima(s, p):
                dve.wait_ge(maxima3[p], 4 * s + 4)
                to = AUGW[p][:, :, :].rearrange("q h (j r) -> q h j r", r=QUAD)
                dve.tensor_copy(to[:, :, :, MAXROW], NM3[p][:, :, :]).then_inc(max_high[p], 1)
                dve.wait_ge(max_high[p], s + 1)
                dve.tensor_tensor(to[:, :, :, MAXROW + 1], NM3[p][:, :, :],
                                  to[:, :, :, MAXROW].bitcast(f32), ALU.subtract)\
                    .then_inc(max_parts[p], 1)

            def add_max_rows(s, p):
                dve.wait_ge(a_full[p], A_ITEM[("aug", s)] + 1)
                if s > 0:
                    dve.wait_ge(scores3[p], 2 * s)
                dve.scalar_tensor_tensor(QSA[p][:, :], QKS[p][s % 2][:, 0, :].bitcast(f32),
                                         col("keep_rows"), bank_a[p][:, 0:N], ALU.mult, ALU.add)\
                    .then_inc(aug_out[p], 1)

            def divide3(b, p):
                item = A_ITEM[("turn", b)]
                dve.wait_ge(a_full[p], item + 1)
                src = bank_a[p].rearrange("q (i j r) -> q i j r", i=4, r=QUAD)
                dve.reciprocal(R3[p][:, :, :], src[:, :, :, HD]).then_inc(recips3[p], 1)
                dve.wait_ge(recips3[p], b + 1)
                for half in range(2):
                    d = dve.tensor_tensor(
                        ON[p][:, half, b, :].rearrange("q (i j d) -> q i j d", i=2, d=HD),
                        src[:, 2 * half:2 * half + 2, :, 0:HD],
                        R3[p][:, 2 * half:2 * half + 2, :].unsqueeze(3).broadcast_to([P, 2, HPG, HD]),
                        ALU.mult)
                d.then_inc(on_out[p], 1)

            statistics(0)
            residual(2, 1)
            normalise(0)
            statistics(1)
            global_feature(0)
            low_parts(0)
            values3(0)
            normalise(1)
            global_feature(1)
            low_parts(1)
            values3(1)
            for s in range(4):
                for j in range(HPG):
                    for p in R:
                        maxima_of(s, j, p)
                for p in R:
                    parts_of_maxima(s, p)
                for p in R:
                    add_max_rows(s, p)
                if s == 2:
                    for p in R:
                        divide3(0, p)
            for p in R:
                divide3(1, p)
            for p in R:
                dve.wait_ge(a_full[p], A_ITEM[("out",)] + 1)
                dve.scalar_tensor_tensor(Y[p][:, :], bank_a[p][:, 0:N], GM[p][:, 1:2], X[p][:, :],
                                         ALU.add, ALU.add).then_inc(y_out[p], 1)


def packed(i):
    where, _, width = places()
    pack = np.zeros((P, width), np.float32)

    def put(name, t):
        a, n = where[name]
        pack[:t.shape[0], a:a + t.shape[1]] = t

    def both(name, wt):
        a, _ = where[name]
        for b in range(2):
            pack[b * C:(b + 1) * C, a + b * C:a + b * C + wt.shape[1]] = wt

    def column(name, v):
        pack[:, where["cols"][0] + COLS.index(name)] = v

    both("wq0", i["L0_conv_Wq"].T)
    both("wk0", i["L0_conv_Wk"].T)
    both("wv0", i["L0_conv_Wv"].T)
    both("wv1", i["L1_conv_Wh"].T)
    both("wq2", i["L2_conv_Wq"].T)
    both("wk2", i["L2_conv_Wk"].T)
    both("wv2", i["L2_conv_Wv"].T)
    qkv, qkv_b = i["L3_conv_qkv_w"], i["L3_conv_qkv_b"]
    both("wq3", qkv[0:C].T)
    both("wk3", qkv[C:2 * C].T)
    both("wv3", qkv[2 * C:3 * C].T)
    both("wg3", i["L3_conv_gproj_w"].T)
    both("wp3", i["L3_conv_proj_w"].T)
    a, _ = where["w1"]
    for side, name in enumerate(("L1_conv_Wf", "L1_conv_Wg")):
        for b in range(2):
            at = a + side * C + b * KINDS1 * HID1
            pack[b * C:(b + 1) * C, at:at + KINDS1 * HID1] = np.tile(i[name].T, (1, KINDS1))
    for name, v in (("vb0", i["L0_conv_bv"]), ("vb1", i["L1_conv_bh"]), ("vb3", qkv_b[2 * C:])):
        put(name, np.tile(v, (P, 2)))
    pad = np.zeros(C - HID0, np.float32)
    column("bq0", np.tile(np.concatenate([i["L0_conv_bq"], pad]), 2))
    column("bk0", np.tile(np.concatenate([i["L0_conv_bk"], pad]), 2))
    column("b1", np.concatenate([np.tile(i["L1_conv_bf"], 2 * KINDS1),
                                 np.tile(i["L1_conv_bg"], 2 * KINDS1)]))
    column("gamma1", i["L1_conv_gamma"][0])
    column("gamma2", i["L2_conv_gamma"][0])
    column("bq3", np.tile(qkv_b[0:C], 2))
    column("bk3", np.tile(qkv_b[C:2 * C], 2))
    for name, v in (("gn_w", i["L3_conv_gn_w"]), ("gn_b", i["L3_conv_gn_b"]),
                    ("proj_b", i["L3_conv_proj_b"]), ("gproj_b", i["L3_conv_gproj_b"])):
        column(name, np.tile(v, 2))
    rows = np.arange(P)
    column("low1", np.concatenate([np.isin(rows[:C] // HID1 % KINDS1, Q_LOW),
                                   np.isin(rows[:C] // HID1 % KINDS1, K_LOW)]))
    column("ones_rows", (rows % QUAD == MAXROW) | (rows % QUAD == MAXROW + 1))
    column("keep_rows", rows % QUAD < MAXROW)
    put("ident", np.eye(P))
    put("fold", np.eye(C)[rows % C])
    put("gavg", (rows[:, None] // GROUP == rows[None, :] // GROUP) / GROUP)
    return pack


def kernel(**inputs):
    import concourse.bacc as bacc
    from concourse.bass_utils import run_bass_kernel_spmd

    inputs = {k: np.asarray(v) for k, v in inputs.items()}
    arrays = {"x": np.ascontiguousarray(inputs["x"]), "pack": packed(inputs)}
    nc = bacc.Bacc("TRN2", target_bir_lowering=False, num_devices=1)
    args = [nc.dram_tensor(n, a.shape, mybir.dt.from_np(a.dtype), kind="ExternalInput").ap()
            for n, a in arrays.items()]
    args.append(nc.dram_tensor("out", (B, C, 16, 16), mybir.dt.float32, kind="ExternalOutput").ap())
    conv_attention_chain(nc, *args)
    return run_bass_kernel_spmd(nc, [arrays], core_ids=[0]).results[0]["out"]
```

```python
from contextlib import ExitStack

import numpy as np
import concourse.bass as bass
from concourse import mybir

B, C, N = 4, 64, 256
PAIRS = 2
P = 128
HALF = N // 2
HID0 = 32
HID1 = 8
HEADS, HD = 8, 8
GROUP = 2
KINDS1 = 4
KINDS3 = 3
Q_LOW = (2, 3)
K_LOW = (1, 3)
QUAD = 32
MAXROW = KINDS3 * HD
HPG = P // QUAD
EPS = 1e-5

GROUPS = [
    [("wq0", P), ("wk0", P), ("wv0", P), ("vb0", P), ("cols", 16)],
    [("ident", P), ("w1", P), ("wv1", P), ("vb1", P)],
    [("wq2", P), ("wk2", P), ("wv2", P), ("fold", C), ("gavg", P), ("heads", HPG)],
    [("wq3", P), ("wk3", P), ("wv3", P), ("vb3", P), ("wg3", P), ("wp3", P)],
]
COLS = ["bq0", "bk0", "b1", "low1", "gamma1", "gamma2", "bq3", "bk3", "ones_rows",
        "gn_w", "gn_b", "proj_b", "gproj_b"]


def places():
    at, where, spans = 0, {}, []
    for group in GROUPS:
        first = at
        for name, width in group:
            where[name] = (at, width)
            at += width
        spans.append((first, at))
    return where, spans, at


def layer3_bank_items():
    a, bc = [], [("stacks", 0)]
    for s in range(5):
        if s > 0:
            bc.append(("score_t", s - 1, 0))
        if s < 3:
            bc.append(("stacks", s + 1))
        if s > 0:
            bc.append(("score_t", s - 1, 1))
        if s < 4:
            a += [("score", s, j) for j in range(HPG)] + [("aug", s)]
        if s == 2:
            a.append(("turn", 0))
    return a + [("turn", 1), ("back",), ("out",)], bc


def conv_attention_chain(nc: bass.Bass, x: bass.AP, pack: bass.AP, out: bass.AP):
    f32, f32r = mybir.dt.float32, mybir.dt.float32r
    ALU, ACT, AX = mybir.AluOpType, mybir.ActivationFunctionType, mybir.AxisListType
    where, spans, width = places()
    x_pairs = x.rearrange("(p b) c h w -> p (b c) (h w)", p=PAIRS)
    out_pairs = out.rearrange("(p b) c h w -> p (b c) (h w)", p=PAIRS)
    A_ORDER, BC_ORDER = layer3_bank_items()
    A_ITEM = {item: n for n, item in enumerate(A_ORDER)}
    BC_ITEM = {item: n for n, item in enumerate(BC_ORDER)}
    R = range(PAIRS)

    with ExitStack() as ctx:
        def sb(name, shape, dt=f32):
            return ctx.enter_context(nc.sbuf_tensor(name, shape, dt))

        def pair_sb(name, shape, dt=f32):
            return [sb(f"{name}{p}", shape, dt) for p in R]

        def pair_sem(name):
            return [ctx.enter_context(nc.semaphore(f"{name}{p}")) for p in R]

        W = sb("W", [P, width])

        def w(name):
            a, n = where[name]
            return W[:, a:a + n]

        def col(name):
            a = where["cols"][0] + COLS.index(name)
            return W[:, a:a + 1]

        ident = w("ident")
        ident_r = sb("ident_r", [P, P], f32r)
        low_bias1 = sb("low_bias1", [P, 1])
        X = pair_sb("X", [P, N])
        Qs = pair_sb("Q", [P, N])
        Ks = pair_sb("K", [P, 2, N])
        V = pair_sb("V", [P, 2, P])
        VS = pair_sb("VS", [P, 2, P])
        M1 = pair_sb("M1", [P, N], f32r)
        F1 = pair_sb("F1", [C, N], f32r)
        G1 = pair_sb("G1", [C, N], f32r)
        NM = [[sb(f"NM{p}{b}", [P, 2]) for b in range(2)] for p in R]
        SUM = [[sb(f"SUM{p}{b}", [P, 2]) for b in range(2)] for p in R]
        RS = [[sb(f"RS{p}{b}", [P, 2]) for b in range(2)] for p in R]
        E = [[sb(f"E{p}{b}", [P, 2, N]) for b in range(2)] for p in R]
        ET = [[sb(f"ET{p}{b}", [P, 2, N]) for b in range(2)] for p in R]
        ST6 = pair_sb("ST6", [P, 6])
        MV = pair_sb("MV", [P, 2])
        GM = pair_sb("GM", [P, 8])
        half_pow = sb("half_pow", [P, 1])
        XN = pair_sb("XN", [P, N])
        QH, QL = pair_sb("QH", [P, N], f32r), pair_sb("QL", [P, N], f32r)
        KH, KL = pair_sb("KH", [P, N], f32r), pair_sb("KL", [P, N], f32r)
        sel = {k: sb(f"sel_{k}", [P, HEADS, QUAD], f32r) for k in ("qh", "ql", "kh", "kl")}
        QKS = [[sb(f"QKS{p}{i}", [P, 2, N], f32r) for i in range(3)] for p in R]
        KM = [[sb(f"KM{p}{i}", [P, HPG, N], f32r) for i in range(3)] for p in R]
        QSA = pair_sb("QSA", [P, N], f32r)
        NM3 = pair_sb("NM3", [P, 2, HPG])
        AUGW = pair_sb("AUGW", [P, 2, P], f32r)
        E3 = [[[sb(f"E3{p}{i}{t}", [P, 2, 2, N]) for t in range(2)] for i in range(2)] for p in R]
        VA = [[sb(f"VA{p}{b}", [P, 2, HEADS, QUAD]) for b in range(2)] for p in R]
        OS = pair_sb("OS", [P, 2, N])
        R3 = pair_sb("R3", [P, 4, HPG])
        ON = pair_sb("ON", [P, 2, 2, C])
        OT = pair_sb("OT", [P, N])
        Y = pair_sb("Y", [P, N])

        PS = [ctx.enter_context(nc.psum_tensor(f"PS{p}", [P, 2048], f32)) for p in R]
        bank_a = [PS[p][:, 0:512] for p in R]
        bank_b = [PS[p][:, 512:1024] for p in R]
        bank_c = [PS[p][:, 1024:1536] for p in R]
        bank_d = [PS[p][:, 1536:2048] for p in R]
        bank_bc = [PS[p][:, 512:1536] for p in R]

        x_loaded = pair_sem("x_loaded")
        w_loaded = [ctx.enter_context(nc.semaphore(f"w_loaded{g}")) for g in range(len(GROUPS))]
        prep_vector = ctx.enter_context(nc.semaphore("prep_vector"))
        prep_pool = ctx.enter_context(nc.semaphore("prep_pool"))
        q_made, k_made, v_made = pair_sem("q_made"), pair_sem("k_made"), pair_sem("v_made")
        q_out, k_out, v_out = pair_sem("q_out"), pair_sem("k_out"), pair_sem("v_out")
        high_out = pair_sem("high_out")
        scores = pair_sem("scores")
        maxima = pair_sem("maxima")
        exps = pair_sem("exps")
        recips = pair_sem("recips")
        divided = pair_sem("divided")
        turned = pair_sem("turned")
        turned_out = pair_sem("turned_out")
        turned_out1 = pair_sem("turned_out1")
        mixed = pair_sem("mixed")
        x_new = pair_sem("x_new")
        stat = pair_sem("stat")
        group_mean, rstd, xn_out, gfeat_made = (pair_sem(n) for n in
                                                ("group_mean", "rstd", "xn_out", "gfeat_made"))
        q_high, q_low, k_high, k_low = (pair_sem(n) for n in ("q_high", "q_low", "k_high", "k_low"))
        a_full, bc_full = pair_sem("a_full"), pair_sem("bc_full")
        maxima3, max_high = pair_sem("maxima3"), pair_sem("max_high")
        max_parts, aug_out = pair_sem("max_parts"), pair_sem("aug_out")
        stack_out, km_out = pair_sem("stack_out"), pair_sem("km_out")
        exps3, mixed3 = pair_sem("exps3"), pair_sem("mixed3")
        o_out, recips3, on_out, ot_out = (pair_sem(n) for n in ("o_out", "recips3", "on_out", "ot_out"))
        y_out, stored = pair_sem("y_out"), pair_sem("stored")

        block = ctx.enter_context(nc.Block())

        @block.sync
        def _(sp):
            sp.dma_start(X[0][:, :], x_pairs[0]).then_inc(x_loaded[0], 16)
            for g, (a, z) in enumerate(spans):
                sp.dma_start(W[:, a:z], pack[:, a:z]).then_inc(w_loaded[g], 16)
                if g == 0:
                    sp.dma_start(X[1][:, :], x_pairs[1]).then_inc(x_loaded[1], 16)
            for p in R:
                sp.wait_ge(y_out[p], 1)
                sp.dma_start(out_pairs[p], Y[p][:, :]).then_inc(stored[p], 16)
            for p in R:
                sp.wait_ge(stored[p], 16)

        ZEROED = 4 * PAIRS + len(sel) + 1
        PREPARED = ZEROED + 2 * PAIRS + 1 + 2 * KINDS3

        @block.gpsimd
        def _(pool):
            for p in R:
                pool.memset(Ks[p][:, :, :], 0.0).then_inc(prep_pool, 1)
            for p in R:
                pool.memset(AUGW[p][:, :, :].bitcast(f32), 0.0).then_inc(prep_pool, 1)
                for b in range(2):
                    pool.memset(VA[p][b][:, :, :, :], 0.0).then_inc(prep_pool, 1)
            for k in sel:
                pool.memset(sel[k][:, :, :].bitcast(f32), 0.0).then_inc(prep_pool, 1)
            pool.memset(half_pow[:, :], -0.5).then_inc(prep_pool, 1)
            pool.wait_ge(prep_pool, ZEROED)
            for p in R:
                for b in range(2):
                    pool.memset(VA[p][b][:, :, :, HD:HD + 1], 1.0).then_inc(prep_pool, 1)
            pool.wait_ge(w_loaded[1], 16)
            pool.wait_ge(w_loaded[2], 16)
            pool.tensor_copy(ident_r[:, :], ident).then_inc(prep_pool, 1)
            fold = w("fold").rearrange("p (h d) -> p h d", d=HD)
            for side, low in (("q", Q_LOW), ("k", K_LOW)):
                for kind in range(KINDS3):
                    part = side + ("l" if kind in low else "h")
                    pool.tensor_copy(sel[part][:, :, kind * HD:(kind + 1) * HD], fold)\
                        .then_inc(prep_pool, 1)
            for p in R:
                pool.wait_ge(stat[p], 5)
                pool.tensor_tensor(GM[p][:, 3:4], GM[p][:, 2:3], half_pow[:, :], ALU.pow)\
                    .then_inc(rstd[p], 1)
            for s in range(4):
                for p in R:
                    pool.wait_ge(stack_out[p], 2 * s + 2)
                    if s >= 3:
                        pool.wait_ge(bc_full[p], BC_ITEM[("score_t", s - 3, 1)] + 1)
                    pool.tensor_tensor(
                        KM[p][s % 3][:, :, :],
                        QKS[p][s % 3][:, 1:2, :].bitcast(f32).broadcast_to([P, HPG, N]),
                        w("heads").unsqueeze(2).broadcast_to([P, HPG, N]), ALU.mult)\
                        .then_inc(km_out[p], 1)


        @block.tensor
        def _(pe):
            def halves(t, rows, half):
                return t[rows, half * HALF:(half + 1) * HALF]

            def values(p, lhs, weights):
                for half in range(2):
                    mm = pe.matmul(bank_c[p][:, half * P:(half + 1) * P],
                                   lhs[:, half * HALF:(half + 1) * HALF], weights,
                                   start=True, stop=True)
                mm.then_inc(v_made[p], 1)

            def project(layer, p):
                if layer == 0:
                    pe.wait_ge(x_loaded[p], 16)
                    if p == 0:
                        pe.wait_ge(w_loaded[0], 16)
                else:
                    if p == 0:
                        pe.wait_ge(w_loaded[layer], 16)
                    pe.wait_ge(x_new[p], layer)
                if layer == 1:
                    pe.matmul(bank_a[p][:, 0:N], w("w1"), X[p][:, :], start=True, stop=True)\
                        .then_inc(q_made[p], 1)
                    values(p, X[p], w("wv1"))
                    return
                pe.matmul(bank_a[p][:, 0:N], w(f"wq{layer}"), X[p][:, :], start=True, stop=True)\
                    .then_inc(q_made[p], 1)
                pe.matmul(bank_b[p][:, 0:N], w(f"wk{layer}"), X[p][:, :], start=True, stop=True)\
                    .then_inc(k_made[p], 1)
                values(p, X[p], w(f"wv{layer}"))

            def score(layer, p):
                pe.wait_ge(q_out[p], layer + 1)
                pe.wait_ge(k_out[p], layer + 1)
                for b, bank in enumerate((bank_a[p], bank_b[p])):
                    if layer == 1:
                        rows = slice(b * QUAD, (b + 1) * QUAD)
                        lhs, rhs = F1[p], G1[p][rows, :]
                    else:
                        rows = slice(0, P)
                        lhs, rhs = Qs[p], Ks[p][:, b, :]
                    for half in range(2):
                        mm = pe.matmul(bank[:, half * N:(half + 1) * N], halves(lhs, rows, half),
                                       rhs, start=True, stop=True)
                    mm.then_inc(scores[p], 1)

            def turn(layer, p):
                for b, bank in enumerate((bank_a[p], bank_b[p])):
                    pe.wait_ge(divided[p], 2 * layer + b + 1)
                    if layer == 0 and p == 0 and b == 0:
                        pe.wait_ge(w_loaded[1], 16)
                    for m in range(2):
                        for n in range(2):
                            tp = pe.transpose(bank[:, m * N + n * HALF:m * N + (n + 1) * HALF],
                                              E[p][b][:, n, m * HALF:(m + 1) * HALF], ident)
                    tp.then_inc(turned[p], 1)

            def mix(layer, p):
                pe.wait_ge(v_out[p], layer + 1)
                if layer == 1:
                    pe.wait_ge(divided[p], 4)
                else:
                    pe.wait_ge(turned_out[p], layer // 2 + 1)
                    pe.wait_ge(turned_out1[p], layer // 2 + 1)
                lhs, rhs = (VS[p], E[p]) if layer == 1 else (V[p], ET[p])
                for m in range(2):
                    for b in range(2):
                        mm = pe.matmul(bank_c[p][b * C:(b + 1) * C, 0:N],
                                       lhs[:, m, b * C:(b + 1) * C], rhs[b][:, m, :],
                                       start=(m == 0), stop=(m == 1))
                mm.then_inc(mixed[p], 1)

            for layer in range(3):
                project(layer, 0)
                if layer > 0:
                    mix(layer - 1, 1)
                score(layer, 0)
                project(layer, 1)
                if layer != 1:
                    turn(layer, 0)
                score(layer, 1)
                mix(layer, 0)
                if layer != 1:
                    turn(layer, 1)

            def group_means(p):
                pe.wait_ge(stat[p], 2)
                pe.matmul(bank_d[p][:, 0:2], w("gavg"), MV[p][:, :], start=True, stop=True)\
                    .then_inc(group_mean[p], 1)

            def project3(p):
                if p == 0:
                    pe.wait_ge(w_loaded[3], 16)
                pe.wait_ge(xn_out[p], 1)
                pe.matmul(bank_d[p][:, 0:1], w("wg3"), GM[p][:, 6:7], start=True, stop=True)\
                    .then_inc(gfeat_made[p], 1)
                pe.matmul(bank_a[p][:, 0:N], w("wq3"), XN[p][:, :], start=True, stop=True)\
                    .then_inc(q_made[p], 1)
                pe.matmul(bank_b[p][:, 0:N], w("wk3"), XN[p][:, :], start=True, stop=True)\
                    .then_inc(k_made[p], 1)
                values(p, XN[p], w("wv3"))

            def a_turn(p, item):
                if A_ITEM[item] == 0:
                    pe.wait_ge(q_low[p], 1)
                    return
                name, *at = A_ORDER[A_ITEM[item] - 1]
                if name == "score":
                    pe.wait_ge(maxima3[p], HPG * at[0] + at[1] + 1)
                elif name == "aug":
                    pe.wait_ge(aug_out[p], at[0] + 1)
                elif name == "turn":
                    pe.wait_ge(on_out[p], at[0] + 1)
                else:
                    pe.wait_ge(ot_out[p], 1)

            def bc_turn(p, item):
                if BC_ITEM[item] == 0:
                    pe.wait_ge(k_low[p], 1)
                    return
                name, *at = BC_ORDER[BC_ITEM[item] - 1]
                if name == "stacks":
                    pe.wait_ge(stack_out[p], 2 * at[0] + 2)
                else:
                    pe.wait_ge(exps3[p], 2 * at[0] + at[1] + 1)
                if item == ("score_t", 0, 0):
                    pe.wait_ge(v_out[p], 4)

            def stacks(s, p):
                b, g = divmod(s, 2)
                rows = slice(b * C, (b + 1) * C)
                bc_turn(p, ("stacks", s))
                if s == 0:
                    pe.wait_ge(prep_pool, PREPARED)
                    pe.wait_ge(q_high[p], 1)
                    pe.wait_ge(q_low[p], 1)
                    pe.wait_ge(k_high[p], 1)
                for i, (side, hi, lo) in enumerate((("q", QH, QL), ("k", KH, KL))):
                    for part, t in (("h", hi), ("l", lo)):
                        lhs = sel[side + part][rows, g * HPG:(g + 1) * HPG, :]
                        mm = pe.matmul(bank_b[p][:, i * N:(i + 1) * N],
                                       lhs.rearrange("c h r -> c (h r)"), t[p][rows, :],
                                       start=(part == "h"), stop=(part == "l"))
                mm.then_inc(bc_full[p], 1)

            def score3(s, j, p):
                a_turn(p, ("score", s, j))
                pe.wait_ge(km_out[p], s + 1)
                for half in range(2):
                    mm = pe.matmul(bank_a[p][:, half * N:(half + 1) * N],
                                   QKS[p][s % 3][:, 0, half * HALF:(half + 1) * HALF],
                                   KM[p][s % 3][:, j, :], start=True, stop=True)
                mm.then_inc(a_full[p], 1)

            def max_rows(s, p):
                a_turn(p, ("aug", s))
                pe.wait_ge(max_parts[p], s + 1)
                for half in range(2):
                    mm = pe.matmul(bank_a[p][:, half * HALF:(half + 1) * HALF],
                                   AUGW[p][:, half, :], ident_r[:, :], start=True, stop=True)
                mm.then_inc(a_full[p], 1)

            def score_t(s, two, p):
                bc_turn(p, ("score_t", s, two))
                if two == 0:
                    pe.wait_ge(aug_out[p], s + 1)
                for m in range(2):
                    for i in range(2):
                        to = (2 * i + m) * N
                        mm = pe.matmul(bank_bc[p][:, to:to + N],
                                       KM[p][s % 3][:, 2 * two + i, m * HALF:(m + 1) * HALF],
                                       QSA[p][:, :], start=True, stop=True)
                mm.then_inc(bc_full[p], 1)

            def mix3(s, m, p):
                b, g = divmod(s, 2)
                pe.wait_ge(exps3[p], 2 * s + 2)
                if s == 2 and m == 0:
                    pe.wait_ge(o_out[p], 1)
                for j in range(HPG):
                    e = E3[p][s % 2][j // 2][:, j % 2, m, :]
                    mm = pe.matmul(bank_d[p][j * QUAD:(j + 1) * QUAD, g * N:(g + 1) * N],
                                   VA[p][b][:, m, g * HPG + j, :], e,
                                   start=(m == 0), stop=(m == 1))
                if m == 1:
                    mm.then_inc(mixed3[p], 1)

            def turn3(b, p):
                a_turn(p, ("turn", b))
                pe.wait_ge(o_out[p], b + 1)
                for half in range(2):
                    for g in range(2):
                        i = 2 * half + g
                        tp = pe.transpose(bank_a[p][:, i * P:(i + 1) * P],
                                          OS[p][:, g, half * HALF:(half + 1) * HALF], ident)
                tp.then_inc(a_full[p], 1)

            def back3(p):
                a_turn(p, ("back",))
                pe.wait_ge(on_out[p], 2)
                for half in range(2):
                    tp = pe.transpose(bank_a[p][:, half * HALF:(half + 1) * HALF],
                                      ON[p][:, half, :, :].rearrange("q b c -> q (b c)"), ident)
                tp.then_inc(a_full[p], 1)

            def out3(p):
                a_turn(p, ("out",))
                pe.wait_ge(ot_out[p], 1)
                pe.matmul(bank_a[p][:, 0:N], w("wp3"), OT[p][:, :], start=True, stop=True)\
                    .then_inc(a_full[p], 1)

            group_means(0)
            mix(2, 1)
            project3(0)
            group_means(1)
            stacks(0, 0)
            project3(1)
            stacks(0, 1)
            for s in range(5):
                now, before = s < 4, s > 0
                for p in R:
                    if now:
                        score3(s, 0, p)
                    if before:
                        score_t(s - 1, 0, p)
                for p in R:
                    if now:
                        score3(s, 1, p)
                    if s < 3:
                        stacks(s + 1, p)
                for p in R:
                    if now:
                        score3(s, 2, p)
                    if before:
                        score_t(s - 1, 1, p)
                for p in R:
                    if now:
                        score3(s, 3, p)
                    if before:
                        mix3(s - 1, p, 0)
                for p in R:
                    if now:
                        max_rows(s, p)
                    if before:
                        mix3(s - 1, p, 1)
                if s == 2:
                    for p in R:
                        turn3(0, p)
            for step in (lambda p: turn3(1, p), back3, out3):
                for p in R:
                    step(p)

        @block.scalar
        def _(act):
            def queries(layer, p):
                if layer == 0 and p == 0:
                    act.wait_ge(prep_vector, 1)
                act.wait_ge(q_made[p], layer + 1)
                if layer == 0:
                    act.activation(Qs[p][:, :], bank_a[p][:, 0:N], ACT.Identity, bias=col("bq0"))\
                        .then_inc(q_out[p], 1)
                elif layer == 1:
                    act.activation(M1[p][:, :], bank_a[p][:, 0:N], ACT.Identity,
                                   bias=low_bias1[:, :], scale=col("low1")).then_inc(high_out[p], 1)
                else:
                    act.activation(Qs[p][:, :], bank_a[p][:, 0:N], ACT.Copy).then_inc(q_out[p], 1)
                    act.wait_ge(v_made[p], 3)
                    act.activation(V[p][:, :, :].rearrange("t h c -> t (h c)"), bank_c[p][:, 0:N],
                                   ACT.Copy).then_inc(v_out[p], 1)

            def exponents(layer, p):
                for b, bank in enumerate((bank_a[p], bank_b[p])):
                    act.wait_ge(maxima[p], 2 * layer + b + 1)
                    for half in range(2):
                        e = act.activation(E[p][b][:, half, :], bank[:, half * N:(half + 1) * N],
                                           ACT.Exp, bias=NM[p][b][:, half:half + 1],
                                           accum_out=SUM[p][b][:, half:half + 1])
                    e.then_inc(exps[p], 1)

            def turned_copy(layer, p):
                act.wait_ge(turned[p], 2 * (layer // 2) + 1)
                act.activation(ET[p][0][:, :, :].rearrange("m h n -> m (h n)"), bank_a[p][:, :],
                               ACT.Copy).then_inc(turned_out[p], 1)

            for layer in range(3):
                queries(layer, 0)
                exponents(layer, 0)
                queries(layer, 1)
                if layer != 1:
                    turned_copy(layer, 0)
                exponents(layer, 1)
                if layer != 1:
                    turned_copy(layer, 1)

            def high_parts(p):
                act.wait_ge(q_made[p], 4)
                act.activation(QH[p][:, :], bank_a[p][:, 0:N], ACT.Identity, bias=col("bq3"))\
                    .then_inc(q_high[p], 1)
                act.wait_ge(k_made[p], 3)
                act.wait_ge(stat[p], 11)
                act.activation(KH[p][:, :], bank_b[p][:, 0:N], ACT.Identity, bias=GM[p][:, 2:3])\
                    .then_inc(k_high[p], 1)

            def stack_copy(s, p):
                act.wait_ge(bc_full[p], BC_ITEM[("stacks", s)] + 1)
                if s >= 3:
                    act.wait_ge(bc_full[p], BC_ITEM[("score_t", s - 3, 1)] + 1)
                act.activation(QKS[p][s % 3][:, 1, :], bank_b[p][:, N:2 * N], ACT.Identity,
                               bias=col("ones_rows")).then_inc(stack_out[p], 1)
                act.activation(QKS[p][s % 3][:, 0, :], bank_b[p][:, 0:N], ACT.Copy)\
                    .then_inc(stack_out[p], 1)

            def exps_t(s, two, p):
                act.wait_ge(bc_full[p], BC_ITEM[("score_t", s, two)] + 1)
                if s >= 2:
                    act.wait_ge(mixed3[p], s - 1)
                act.activation(E3[p][s % 2][two][:, :, :, :].rearrange("k j m q -> k (j m q)"),
                               bank_bc[p][:, :], ACT.Exp, scale=float(HD) ** -0.5)\
                    .then_inc(exps3[p], 1)

            def o_copy(b, p):
                act.wait_ge(mixed3[p], 2 * (b + 1))
                act.activation(OS[p][:, :, :].rearrange("r g n -> r (g n)"), bank_d[p][:, :],
                               ACT.Copy).then_inc(o_out[p], 1)

            for p in R:
                high_parts(p)
                stack_copy(0, p)
            for s in range(5):
                for p in R:
                    if s > 0:
                        exps_t(s - 1, 0, p)
                for p in R:
                    if s < 3:
                        stack_copy(s + 1, p)
                for p in R:
                    if s > 0:
                        exps_t(s - 1, 1, p)
                if s in (2, 4):
                    for p in R:
                        o_copy(s // 2 - 1, p)
            for p in R:
                act.wait_ge(a_full[p], A_ITEM[("back",)] + 1)
                act.activation(OT[p][:, :], bank_a[p][:, 0:N], ACT.Copy).then_inc(ot_out[p], 1)

        @block.vector
        def _(dve):
            dve.wait_ge(w_loaded[0], 16)
            dve.tensor_tensor(low_bias1[:, :], col("b1"), col("low1"), ALU.mult)\
                .then_inc(prep_vector, 1)

            def keys_and_values(layer, p):
                if layer == 1:
                    dve.wait_ge(high_out[p], 1)
                    for dst, rows, done in ((F1, slice(0, C), q_out), (G1, slice(C, P), k_out)):
                        dve.scalar_tensor_tensor(dst[p][:, :], bank_a[p][rows, 0:N],
                                                 col("b1")[rows, :], M1[p][rows, :].bitcast(f32),
                                                 ALU.add, ALU.subtract).then_inc(done[p], 1)
                else:
                    dve.wait_ge(k_made[p], layer // 2 + 1)
                    if layer == 0:
                        dve.wait_ge(prep_pool, p + 1)
                    for b in range(2):
                        rows = slice(b * C, (b + 1) * C)
                        if layer == 0:
                            k = dve.tensor_scalar(Ks[p][rows, b, :], bank_b[p][rows, 0:N],
                                                  col("bk0")[rows, :], None, ALU.add)
                        else:
                            k = dve.tensor_copy(Ks[p][rows, b, :], bank_b[p][rows, 0:N])
                    k.then_inc(k_out[p], 1)
                if layer < 2:
                    dve.wait_ge(v_made[p], layer + 1)
                    bias = w(f"vb{layer}").unsqueeze(1).broadcast_to([P, 2, P])
                    dve.tensor_tensor(V[p][:, :, :], bank_c[p][:, 0:N].rearrange(
                        "t (h c) -> t h c", h=2), bias, ALU.add).then_inc(v_out[p], 1)

            def row_maxima(layer, p):
                for b, bank in enumerate((bank_a[p], bank_b[p])):
                    i = 2 * layer + b
                    dve.wait_ge(scores[p], i + 1)
                    dve.tensor_reduce(NM[p][b][:, :], bank.rearrange("r (h c) -> r h c", h=2), AX.X,
                                      ALU.max, negate=True).then_inc(maxima[p], 1)

            def divide(layer, p):
                for b in range(2):
                    i = 2 * layer + b
                    dve.wait_ge(exps[p], i + 1)
                    dve.reciprocal(RS[p][b][:, :], SUM[p][b][:, :]).then_inc(recips[p], 1)
                    dve.wait_ge(recips[p], i + 1)
                    if layer == 1:
                        cols = slice(b * C, (b + 1) * C)
                        dve.wait_ge(v_out[p], 2)
                        dve.tensor_tensor(VS[p][:, :, cols], V[p][:, :, cols],
                                          RS[p][b][:, :].unsqueeze(2).broadcast_to([P, 2, C]),
                                          ALU.mult).then_inc(divided[p], 1)
                    else:
                        for half in range(2):
                            d = dve.tensor_scalar(E[p][b][:, half, :], E[p][b][:, half, :],
                                                  RS[p][b][:, half:half + 1], None, ALU.mult)
                        d.then_inc(divided[p], 1)

            def turned_copy(layer, p):
                dve.wait_ge(turned[p], 2 * (layer // 2) + 2)
                dve.tensor_copy(ET[p][1][:, :, :].rearrange("m h n -> m (h n)"), bank_b[p][:, :])\
                    .then_inc(turned_out1[p], 1)

            def residual(layer, p):
                dve.wait_ge(mixed[p], layer + 1)
                if layer == 0:
                    dve.tensor_tensor(X[p][:, :], bank_c[p][:, 0:N], X[p][:, :], ALU.add)\
                        .then_inc(x_new[p], 1)
                else:
                    dve.scalar_tensor_tensor(X[p][:, :], bank_c[p][:, 0:N], col(f"gamma{layer}"),
                                             X[p][:, :], ALU.mult, ALU.add).then_inc(x_new[p], 1)

            for layer in range(3):
                keys_and_values(layer, 0)
                if layer > 0:
                    residual(layer - 1, 1)
                row_maxima(layer, 0)
                divide(layer, 0)
                keys_and_values(layer, 1)
                row_maxima(layer, 1)
                if layer != 1:
                    turned_copy(layer, 0)
                residual(layer, 0)
                divide(layer, 1)
                if layer != 1:
                    turned_copy(layer, 1)

            def small(p, n, ins):
                ins.then_inc(stat[p], 1)
                dve.wait_ge(stat[p], n)

            def statistics(p):
                dve.wait_ge(x_new[p], 3)
                small(p, 1, dve.bn_stats(ST6[p][:, :], X[p][:, :]))
                small(p, 2, dve.bn_aggr(MV[p][:, :], ST6[p][:, :]))

            def normalise(p):
                m = GM[p]
                dve.wait_ge(group_mean[p], 1)
                small(p, 3, dve.tensor_tensor(m[:, 0:1], bank_d[p][:, 0:1], MV[p][:, 0:1],
                                              ALU.subtract))
                small(p, 4, dve.tensor_tensor(m[:, 1:2], m[:, 0:1], m[:, 0:1], ALU.mult))
                small(p, 5, dve.scalar_tensor_tensor(m[:, 2:3], bank_d[p][:, 1:2], EPS, m[:, 1:2],
                                                     ALU.add, ALU.add))
                dve.wait_ge(rstd[p], 1)
                small(p, 6, dve.tensor_tensor(m[:, 4:5], m[:, 3:4], col("gn_w"), ALU.mult))
                small(p, 7, dve.tensor_tensor(m[:, 7:8], bank_d[p][:, 0:1], m[:, 4:5], ALU.mult))
                small(p, 8, dve.tensor_tensor(m[:, 5:6], col("gn_b"), m[:, 7:8], ALU.subtract))
                small(p, 9, dve.scalar_tensor_tensor(m[:, 6:7], MV[p][:, 0:1], m[:, 4:5],
                                                     m[:, 5:6], ALU.mult, ALU.add))
                dve.tensor_scalar(XN[p][:, :], X[p][:, :], m[:, 4:5], m[:, 5:6], ALU.mult, ALU.add)\
                    .then_inc(xn_out[p], 1)

            def global_feature(p):
                m = GM[p]
                dve.wait_ge(gfeat_made[p], 1)
                small(p, 10, dve.tensor_scalar(m[:, 0:1], bank_d[p][:, 0:1], col("gproj_b"), 0.1,
                                               ALU.add, ALU.mult))
                small(p, 11, dve.tensor_tensor(m[:, 2:3], m[:, 0:1], col("bk3"), ALU.add))
                small(p, 12, dve.tensor_tensor(m[:, 1:2], m[:, 0:1], col("proj_b"), ALU.add))

            def low_parts(p):
                dve.wait_ge(q_high[p], 1)
                dve.scalar_tensor_tensor(QL[p][:, :], bank_a[p][:, 0:N], col("bq3"),
                                         QH[p][:, :].bitcast(f32), ALU.add, ALU.subtract)\
                    .then_inc(q_low[p], 1)
                dve.wait_ge(k_high[p], 1)
                dve.scalar_tensor_tensor(KL[p][:, :], bank_b[p][:, 0:N], GM[p][:, 2:3],
                                         KH[p][:, :].bitcast(f32), ALU.add, ALU.subtract)\
                    .then_inc(k_low[p], 1)

            def values3(p):
                dve.wait_ge(v_made[p], 4)
                if p == 0:
                    dve.wait_ge(prep_pool, PREPARED)
                for b in range(2):
                    src = bank_c[p][:, 0:N].rearrange("t (h b e d) -> t h b e d", h=2, b=2, d=HD)
                    bias = w("vb3")[:, 0:C].rearrange("t (e d) -> t e d", d=HD)
                    v = dve.tensor_tensor(VA[p][b][:, :, :, 0:HD], src[:, :, b],
                                          bias.unsqueeze(1).broadcast_to([P, 2, HEADS, HD]), ALU.add)
                v.then_inc(v_out[p], 1)

            def maxima_of(s, j, p):
                dve.wait_ge(a_full[p], A_ITEM[("score", s, j)] + 1)
                dve.tensor_reduce(NM3[p][:, :, j], bank_a[p].rearrange("q (h k) -> q h k", h=2),
                                  AX.X, ALU.max, negate=True).then_inc(maxima3[p], 1)

            def parts_of_maxima(s, p):
                dve.wait_ge(maxima3[p], 4 * s + 4)
                to = AUGW[p][:, :, :].rearrange("q h (j r) -> q h j r", r=QUAD)
                dve.tensor_copy(to[:, :, :, MAXROW], NM3[p][:, :, :]).then_inc(max_high[p], 1)
                dve.wait_ge(max_high[p], s + 1)
                dve.tensor_tensor(to[:, :, :, MAXROW + 1], NM3[p][:, :, :],
                                  to[:, :, :, MAXROW].bitcast(f32), ALU.subtract)\
                    .then_inc(max_parts[p], 1)

            def add_max_rows(s, p):
                dve.wait_ge(a_full[p], A_ITEM[("aug", s)] + 1)
                if s > 0:
                    dve.wait_ge(bc_full[p], BC_ITEM[("score_t", s - 1, 1)] + 1)
                dve.tensor_tensor(QSA[p][:, :], QKS[p][s % 3][:, 0, :].bitcast(f32),
                                  bank_a[p][:, 0:N], ALU.add)\
                    .then_inc(aug_out[p], 1)

            def divide3(b, p):
                item = A_ITEM[("turn", b)]
                dve.wait_ge(a_full[p], item + 1)
                src = bank_a[p].rearrange("q (i j r) -> q i j r", i=4, r=QUAD)
                dve.reciprocal(R3[p][:, :, :], src[:, :, :, HD]).then_inc(recips3[p], 1)
                dve.wait_ge(recips3[p], b + 1)
                for half in range(2):
                    d = dve.tensor_tensor(
                        ON[p][:, half, b, :].rearrange("q (i j d) -> q i j d", i=2, d=HD),
                        src[:, 2 * half:2 * half + 2, :, 0:HD],
                        R3[p][:, 2 * half:2 * half + 2, :].unsqueeze(3).broadcast_to([P, 2, HPG, HD]),
                        ALU.mult)
                d.then_inc(on_out[p], 1)

            statistics(0)
            residual(2, 1)
            normalise(0)
            statistics(1)
            global_feature(0)
            low_parts(0)
            values3(0)
            normalise(1)
            global_feature(1)
            low_parts(1)
            values3(1)
            for s in range(4):
                for j in range(HPG - 1):
                    for p in R:
                        maxima_of(s, j, p)
                maxima_of(s, HPG - 1, 0)
                parts_of_maxima(s, 0)
                maxima_of(s, HPG - 1, 1)
                parts_of_maxima(s, 1)
                for p in R:
                    add_max_rows(s, p)
                if s == 2:
                    for p in R:
                        divide3(0, p)
            for p in R:
                divide3(1, p)
            for p in R:
                dve.wait_ge(a_full[p], A_ITEM[("out",)] + 1)
                dve.scalar_tensor_tensor(Y[p][:, :], bank_a[p][:, 0:N], GM[p][:, 1:2], X[p][:, :],
                                         ALU.add, ALU.add).then_inc(y_out[p], 1)


def packed(i):
    where, _, width = places()
    pack = np.zeros((P, width), np.float32)

    def put(name, t):
        a, n = where[name]
        pack[:t.shape[0], a:a + t.shape[1]] = t

    def both(name, wt):
        a, _ = where[name]
        for b in range(2):
            pack[b * C:(b + 1) * C, a + b * C:a + b * C + wt.shape[1]] = wt

    def column(name, v):
        pack[:, where["cols"][0] + COLS.index(name)] = v

    both("wq0", i["L0_conv_Wq"].T)
    both("wk0", i["L0_conv_Wk"].T)
    both("wv0", i["L0_conv_Wv"].T)
    both("wv1", i["L1_conv_Wh"].T)
    both("wq2", i["L2_conv_Wq"].T)
    both("wk2", i["L2_conv_Wk"].T)
    both("wv2", i["L2_conv_Wv"].T)
    qkv, qkv_b = i["L3_conv_qkv_w"], i["L3_conv_qkv_b"]
    both("wq3", qkv[0:C].T)
    both("wk3", qkv[C:2 * C].T)
    both("wv3", qkv[2 * C:3 * C].T)
    both("wg3", i["L3_conv_gproj_w"].T)
    both("wp3", i["L3_conv_proj_w"].T)
    a, _ = where["w1"]
    for side, name in enumerate(("L1_conv_Wf", "L1_conv_Wg")):
        for b in range(2):
            at = a + side * C + b * KINDS1 * HID1
            pack[b * C:(b + 1) * C, at:at + KINDS1 * HID1] = np.tile(i[name].T, (1, KINDS1))
    for name, v in (("vb0", i["L0_conv_bv"]), ("vb1", i["L1_conv_bh"]), ("vb3", qkv_b[2 * C:])):
        put(name, np.tile(v, (P, 2)))
    pad = np.zeros(C - HID0, np.float32)
    column("bq0", np.tile(np.concatenate([i["L0_conv_bq"], pad]), 2))
    column("bk0", np.tile(np.concatenate([i["L0_conv_bk"], pad]), 2))
    column("b1", np.concatenate([np.tile(i["L1_conv_bf"], 2 * KINDS1),
                                 np.tile(i["L1_conv_bg"], 2 * KINDS1)]))
    column("gamma1", i["L1_conv_gamma"][0])
    column("gamma2", i["L2_conv_gamma"][0])
    column("bq3", np.tile(qkv_b[0:C], 2))
    column("bk3", np.tile(qkv_b[C:2 * C], 2))
    for name, v in (("gn_w", i["L3_conv_gn_w"]), ("gn_b", i["L3_conv_gn_b"]),
                    ("proj_b", i["L3_conv_proj_b"]), ("gproj_b", i["L3_conv_gproj_b"])):
        column(name, np.tile(v, 2))
    rows = np.arange(P)
    column("low1", np.concatenate([np.isin(rows[:C] // HID1 % KINDS1, Q_LOW),
                                   np.isin(rows[:C] // HID1 % KINDS1, K_LOW)]))
    column("ones_rows", (rows % QUAD == MAXROW) | (rows % QUAD == MAXROW + 1))
    put("heads", rows[:, None] // QUAD == np.arange(HPG))
    put("ident", np.eye(P))
    put("fold", np.eye(C)[rows % C])
    put("gavg", (rows[:, None] // GROUP == rows[None, :] // GROUP) / GROUP)
    return pack


def kernel(**inputs):
    import concourse.bacc as bacc
    from concourse.bass_utils import run_bass_kernel_spmd

    inputs = {k: np.asarray(v) for k, v in inputs.items()}
    arrays = {"x": np.ascontiguousarray(inputs["x"]), "pack": packed(inputs)}
    nc = bacc.Bacc("TRN2", target_bir_lowering=False, num_devices=1)
    args = [nc.dram_tensor(n, a.shape, mybir.dt.from_np(a.dtype), kind="ExternalInput").ap()
            for n, a in arrays.items()]
    args.append(nc.dram_tensor("out", (B, C, 16, 16), mybir.dt.float32, kind="ExternalOutput").ap())
    conv_attention_chain(nc, *args)
    return run_bass_kernel_spmd(nc, [arrays], core_ids=[0]).results[0]["out"]
```

```python
from contextlib import ExitStack

import numpy as np
import concourse.bass as bass
from concourse import mybir

B, C, N = 4, 64, 256
PAIRS = 2
P = 128
HALF = N // 2
HID0 = 32
HID1 = 8
HEADS, HD = 8, 8
GROUP = 2
KINDS1 = 4
KINDS3 = 3
Q_LOW = (2, 3)
K_LOW = (1, 3)
QUAD = 32
MAXROW = KINDS3 * HD
HPG = P // QUAD
EPS = 1e-5

VALUES0 = 4
GROUPS = [
    [("w0", P), ("cols", 16)],
    [("ident", P), ("w1", P), ("wv1", P), ("vb1", P)],
    [("wq2", P), ("wk2", P), ("wv2", P), ("fold", C), ("gavg", P), ("heads", HPG)],
    [("wq3", P), ("wk3", P), ("wv3", P), ("vb3", P), ("wg3", P), ("wp3", P)],
    [("wv0", P), ("vb0", P)],
]
COLS = ["b0", "b1", "low1", "gamma1", "gamma2", "bq3", "bk3", "ones_rows",
        "gn_w", "gn_b", "proj_b", "gproj_b"]


def places():
    at, where, spans = 0, {}, []
    for group in GROUPS:
        first = at
        for name, width in group:
            where[name] = (at, width)
            at += width
        spans.append((first, at))
    return where, spans, at




def layer3_bank_items():
    a, bc = [], [("stacks", 0)]
    for s in range(5):
        if s < 4:
            a.append(("score", s, 0))
        if s > 0:
            a.append(("aug", s - 1))
        if s < 4:
            a += [("score", s, j) for j in range(1, HPG)]
        if s < 3:
            bc.append(("stacks", s + 1))
        if s > 0:
            bc += [("score_t", s - 1, 0), ("score_t", s - 1, 1)]
    return a + [("turn", s) for s in range(4)] + [("back",), ("out",)], bc


def conv_attention_chain(nc: bass.Bass, x: bass.AP, pack: bass.AP, out: bass.AP):
    f32, f32r = mybir.dt.float32, mybir.dt.float32r
    ALU, ACT, AX = mybir.AluOpType, mybir.ActivationFunctionType, mybir.AxisListType
    where, spans, width = places()
    x_pairs = x.rearrange("(p b) c h w -> p (b c) (h w)", p=PAIRS)
    out_pairs = out.rearrange("(p b) c h w -> p (b c) (h w)", p=PAIRS)
    A_ORDER, BC_ORDER = layer3_bank_items()
    A_ITEM = {item: n for n, item in enumerate(A_ORDER)}
    BC_ITEM = {item: n for n, item in enumerate(BC_ORDER)}
    R = range(PAIRS)

    with ExitStack() as ctx:
        def sb(name, shape, dt=f32):
            return ctx.enter_context(nc.sbuf_tensor(name, shape, dt))

        def pair_sb(name, shape, dt=f32):
            return [sb(f"{name}{p}", shape, dt) for p in R]

        def pair_sem(name):
            return [ctx.enter_context(nc.semaphore(f"{name}{p}")) for p in R]

        W = sb("W", [P, width])

        def w(name):
            a, n = where[name]
            return W[:, a:a + n]

        def col(name):
            a = where["cols"][0] + COLS.index(name)
            return W[:, a:a + 1]

        ident = w("ident")
        ident_r = sb("ident_r", [P, P], f32r)
        idle = sb("idle", [P, N], f32r)
        low_bias1 = sb("low_bias1", [P, 1])
        feature_bias = sb("feature_bias", [P, 2])
        X = pair_sb("X", [P, N])
        Qs = pair_sb("Q", [P, N])
        K0s = pair_sb("K0", [2 * HID0, 2, N])
        Ks = pair_sb("K", [P, 2, N])
        V = pair_sb("V", [P, 2, P])
        VS = pair_sb("VS", [P, 2, P])
        M1 = pair_sb("M1", [P, N], f32r)
        F1 = pair_sb("F1", [C, N], f32r)
        G1 = pair_sb("G1", [C, N], f32r)
        NM = [[sb(f"NM{p}{b}", [P, 2]) for b in range(2)] for p in R]
        SUM = [[sb(f"SUM{p}{b}", [P, 2]) for b in range(2)] for p in R]
        RS = [[sb(f"RS{p}{b}", [P, 2]) for b in range(2)] for p in R]
        E = [[sb(f"E{p}{b}", [P, 2, N]) for b in range(2)] for p in R]
        ET = [[sb(f"ET{p}{b}", [P, 2, N]) for b in range(2)] for p in R]
        ST6 = pair_sb("ST6", [P, 6])
        MV = pair_sb("MV", [P, 2])
        GM = pair_sb("GM", [P, 8])
        half_pow = sb("half_pow", [P, 1])
        XN = pair_sb("XN", [P, N])
        QH, QL = pair_sb("QH", [P, N], f32r), pair_sb("QL", [P, N], f32r)
        KH, KL = pair_sb("KH", [P, N], f32r), pair_sb("KL", [P, N], f32r)
        sel = {k: sb(f"sel_{k}", [P, HEADS, QUAD], f32r) for k in ("qh", "ql", "kh", "kl")}
        QKS = [[sb(f"QKS{p}{i}", [P, 2, N], f32r) for i in range(3)] for p in R]
        KM = [[sb(f"KM{p}{i}", [P, HPG, N], f32r) for i in range(3)] for p in R]
        QSA = pair_sb("QSA", [P, N], f32r)
        NM3 = pair_sb("NM3", [P, 2, 2, HPG])
        AUGW = pair_sb("AUGW", [P, 2, P], f32r)
        E3 = [[[sb(f"E3{p}{i}{m}", [P, HPG, N]) for m in range(2)] for i in range(2)] for p in R]
        VA = [[sb(f"VA{p}{b}", [P, 2, HEADS, QUAD]) for b in range(2)] for p in R]
        OS = pair_sb("OS", [P, 2, N])
        R3 = pair_sb("R3", [P, 4, 2, HPG])
        ON = pair_sb("ON", [P, 2, 2, C])
        OT = pair_sb("OT", [P, N])
        Y = pair_sb("Y", [P, N])

        PS = [ctx.enter_context(nc.psum_tensor(f"PS{p}", [P, 2048], f32)) for p in R]
        bank_a = [PS[p][:, 0:512] for p in R]
        bank_b = [PS[p][:, 512:1024] for p in R]
        bank_c = [PS[p][:, 1024:1536] for p in R]
        bank_d = [PS[p][:, 1536:2048] for p in R]
        bank_bc = [PS[p][:, 512:1536] for p in R]

        x_loaded = pair_sem("x_loaded")
        w_loaded = [ctx.enter_context(nc.semaphore(f"w_loaded{g}")) for g in range(len(GROUPS))]
        prep_vector = ctx.enter_context(nc.semaphore("prep_vector"))
        idle_set = ctx.enter_context(nc.semaphore("idle_set"))
        prep_pool = ctx.enter_context(nc.semaphore("prep_pool"))
        q_made, k_made, v_made = pair_sem("q_made"), pair_sem("k_made"), pair_sem("v_made")
        q_out, k_out, v_out = pair_sem("q_out"), pair_sem("k_out"), pair_sem("v_out")
        k_out1 = pair_sem("k_out1")
        high_out = pair_sem("high_out")
        scores = pair_sem("scores")
        maxima = pair_sem("maxima")
        exps = pair_sem("exps")
        recips = pair_sem("recips")
        divided = pair_sem("divided")
        turned = pair_sem("turned")
        turned_out = pair_sem("turned_out")
        turned_out1 = pair_sem("turned_out1")
        mixed = pair_sem("mixed")
        x_new = pair_sem("x_new")
        stat = pair_sem("stat")
        group_mean, rstd, xn_out, gfeat_made = (pair_sem(n) for n in
                                                ("group_mean", "rstd", "xn_out", "gfeat_made"))
        q_high, q_low, k_high, k_low = (pair_sem(n) for n in ("q_high", "q_low", "k_high", "k_low"))
        a_full, bc_full = pair_sem("a_full"), pair_sem("bc_full")
        maxima3, max_high = pair_sem("maxima3"), pair_sem("max_high")
        max_parts, aug_out = pair_sem("max_parts"), pair_sem("aug_out")
        first_keys = pair_sem("first_keys")
        stack_out, km_out = pair_sem("stack_out"), pair_sem("km_out")
        exps3, mixed3 = pair_sem("exps3"), pair_sem("mixed3")
        o_out, recips3 = pair_sem("o_out"), pair_sem("recips3")
        on_out, ot_out = pair_sem("on_out"), pair_sem("ot_out")
        y_out, stored = pair_sem("y_out"), pair_sem("stored")

        block = ctx.enter_context(nc.Block())

        @block.sync
        def _(sp):
            for p in R:
                sp.dma_start(X[p][:, :], x_pairs[p]).then_inc(x_loaded[p], 16)
            for g, (a, z) in enumerate(spans):
                if g not in (0, VALUES0):
                    sp.dma_start(W[:, a:z], pack[:, a:z]).then_inc(w_loaded[g], 16)
            for p in R:
                sp.wait_ge(y_out[p], 1)
                sp.dma_start(out_pairs[p], Y[p][:, :]).then_inc(stored[p], 16)
            for p in R:
                sp.wait_ge(stored[p], 16)

        ZEROED = 5 * PAIRS + len(sel) + 1
        PREPARED = ZEROED + 2 * PAIRS + 1 + 2 * KINDS3

        @block.gpsimd
        def _(pool):
            for p in R:
                pool.memset(K0s[p][:, :, :], 0.0).then_inc(prep_pool, 1)
            for p in R:
                pool.memset(Ks[p][:, :, :], 0.0).then_inc(prep_pool, 1)
            for p in R:
                pool.memset(AUGW[p][:, :, :].bitcast(f32), 0.0).then_inc(prep_pool, 1)
                for b in range(2):
                    pool.memset(VA[p][b][:, :, :, :], 0.0).then_inc(prep_pool, 1)
            for k in sel:
                pool.memset(sel[k][:, :, :].bitcast(f32), 0.0).then_inc(prep_pool, 1)
            pool.memset(half_pow[:, :], -0.5).then_inc(prep_pool, 1)
            pool.wait_ge(prep_pool, ZEROED)
            for p in R:
                for b in range(2):
                    pool.memset(VA[p][b][:, :, :, HD:HD + 1], 1.0).then_inc(prep_pool, 1)
            pool.wait_ge(w_loaded[1], 16)
            pool.wait_ge(w_loaded[2], 16)
            pool.tensor_copy(ident_r[:, :], ident).then_inc(prep_pool, 1)
            fold = w("fold").rearrange("p (h d) -> p h d", d=HD)
            for side, low in (("q", Q_LOW), ("k", K_LOW)):
                for kind in range(KINDS3):
                    part = side + ("l" if kind in low else "h")
                    pool.tensor_copy(sel[part][:, :, kind * HD:(kind + 1) * HD], fold)\
                        .then_inc(prep_pool, 1)

            def group_rstd(p):
                pool.wait_ge(stat[p], 5)
                pool.tensor_tensor(GM[p][:, 3:4], GM[p][:, 2:3], half_pow[:, :], ALU.pow)\
                    .then_inc(rstd[p], 1)

            def head_keys(s, two, p):
                pool.wait_ge(stack_out[p], 2 * s + 1)
                if s >= 3:
                    pool.wait_ge(bc_full[p], BC_ITEM[("score_t", s - 3, 1)] + 1)
                heads = slice(2 * two, 2 * two + 2)
                pool.tensor_tensor(
                    KM[p][s % 3][:, heads, :],
                    QKS[p][s % 3][:, 1:2, :].bitcast(f32).broadcast_to([P, 2, N]),
                    w("heads")[:, heads].unsqueeze(2).broadcast_to([P, 2, N]), ALU.mult)\
                    .then_inc(km_out[p], 1)

            group_rstd(0)
            head_keys(0, 1, 0)
            group_rstd(1)
            head_keys(1, 0, 0)
            head_keys(1, 1, 0)
            head_keys(0, 1, 1)
            for g in range(1, 4):
                for two in range(2):
                    for p in R:
                        if g + 1 - p < 4:
                            head_keys(g + 1 - p, two, p)

        @block.tensor
        def _(pe):
            def keep_clock(n, p):
                for _ in range(n):
                    pe.matmul(bank_d[p][:, 0:N], idle[:, 0:P], idle[:, :], start=True, stop=True)

            def halves(t, rows, half):
                return t[rows, half * HALF:(half + 1) * HALF]

            def values(layer, tokens, p):
                if layer == 0:
                    pe.wait_ge(w_loaded[VALUES0], 16)
                for half in range(2):
                    mm = pe.matmul(bank_c[p][:, half * P:(half + 1) * P],
                                   tokens[:, half * HALF:(half + 1) * HALF], w(f"wv{layer}"),
                                   start=True, stop=True)
                mm.then_inc(v_made[p], 1)

            def project(layer, p):
                if layer == 0:
                    pe.wait_ge(x_loaded[p], 16)
                    if p == 0:
                        pe.wait_ge(w_loaded[0], 16)
                else:
                    if p == 0:
                        pe.wait_ge(w_loaded[layer], 16)
                    pe.wait_ge(x_new[p], layer)
                if layer < 2:
                    pe.matmul(bank_a[p][:, 0:N], w(f"w{layer}"), X[p][:, :], start=True, stop=True)\
                        .then_inc(q_made[p], 1)
                    return
                pe.matmul(bank_a[p][:, 0:N], w(f"wq{layer}"), X[p][:, :], start=True, stop=True)\
                    .then_inc(q_made[p], 1)
                pe.matmul(bank_b[p][:, 0:N], w(f"wk{layer}"), X[p][:, :], start=True, stop=True)\
                    .then_inc(k_made[p], 1)

            def score(layer, b, p):
                pe.wait_ge(q_out[p], layer + 1)
                if layer != 1:
                    pe.wait_ge(k_out1[p], layer // 2 + 1)
                pe.wait_ge(k_out[p], layer + 1)
                if layer == 1:
                    rows = slice(b * QUAD, (b + 1) * QUAD)
                    lhs, rhs = F1[p], G1[p][rows, :]
                else:
                    rows = slice(0, P if layer == 2 else 2 * HID0)
                    lhs, rhs = Qs[p], (Ks if layer == 2 else K0s)[p][:, b, :]
                bank = (bank_a, bank_b)[b][p]
                for half in range(2):
                    mm = pe.matmul(bank[:, half * N:(half + 1) * N], halves(lhs, rows, half),
                                   rhs, start=True, stop=True)
                mm.then_inc(scores[p], 1)

            def turn(layer, b, p):
                bank = (bank_a, bank_b)[b][p]
                pe.wait_ge(divided[p], 2 * layer + b + 1)
                if layer == 0 and p == 0 and b == 0:
                    pe.wait_ge(w_loaded[1], 16)
                for m in range(2):
                    for n in range(2):
                        tp = pe.transpose(bank[:, m * N + n * HALF:m * N + (n + 1) * HALF],
                                          E[p][b][:, n, m * HALF:(m + 1) * HALF], ident)
                tp.then_inc(turned[p], 1)

            def mix(layer, p):
                pe.wait_ge(v_out[p], layer + 1)
                if layer == 1:
                    pe.wait_ge(divided[p], 4)
                else:
                    pe.wait_ge(turned_out[p], layer // 2 + 1)
                    pe.wait_ge(turned_out1[p], layer // 2 + 1)
                lhs, rhs = (VS[p], E[p]) if layer == 1 else (V[p], ET[p])
                for m in range(2):
                    for b in range(2):
                        mm = pe.matmul(bank_c[p][b * C:(b + 1) * C, 0:N],
                                       lhs[:, m, b * C:(b + 1) * C], rhs[b][:, m, :],
                                       start=(m == 0), stop=(m == 1))
                mm.then_inc(mixed[p], 1)

            def group_means(p):
                pe.wait_ge(stat[p], 2)
                pe.matmul(bank_d[p][:, 0:2], w("gavg"), MV[p][:, :], start=True, stop=True)\
                    .then_inc(group_mean[p], 1)

            def project3(p):
                if p == 0:
                    pe.wait_ge(w_loaded[3], 16)
                pe.wait_ge(stat[p], 8)
                pe.matmul(bank_d[p][:, 0:1], w("wg3"), GM[p][:, 6:7], start=True, stop=True)\
                    .then_inc(gfeat_made[p], 1)
                pe.wait_ge(xn_out[p], 1)
                pe.matmul(bank_b[p][:, 0:N], w("wk3"), XN[p][:, :], start=True, stop=True)\
                    .then_inc(k_made[p], 1)
                pe.matmul(bank_a[p][:, 0:N], w("wq3"), XN[p][:, :], start=True, stop=True)\
                    .then_inc(q_made[p], 1)

            def a_turn(p, item):
                if A_ITEM[item] == 0:
                    pe.wait_ge(q_low[p], 1)
                    return
                name, *at = A_ORDER[A_ITEM[item] - 1]
                if name == "score":
                    pe.wait_ge(maxima3[p], HPG * at[0] + at[1] + 1)
                elif name == "aug":
                    pe.wait_ge(aug_out[p], at[0] + 1)
                elif name == "turn":
                    pe.wait_ge(on_out[p], at[0] + 1)
                else:
                    pe.wait_ge(ot_out[p], 1)

            def bc_turn(p, item):
                if BC_ITEM[item] == 0:
                    pe.wait_ge(k_low[p], 1)
                    return
                name, *at = BC_ORDER[BC_ITEM[item] - 1]
                if name == "stacks":
                    pe.wait_ge(stack_out[p], 2 * at[0] + 2)
                else:
                    pe.wait_ge(exps3[p], 2 * at[0] + at[1] + 1)
                if item == ("score_t", 0, 0):
                    pe.wait_ge(v_out[p], 4)

            def stacks(s, p):
                b, g = divmod(s, 2)
                rows = slice(b * C, (b + 1) * C)
                bc_turn(p, ("stacks", s))
                if s == 0:
                    pe.wait_ge(prep_pool, PREPARED)
                for i, side, hi, lo, high, low in ((1, "k", KH, KL, k_high, k_low),
                                                   (0, "q", QH, QL, q_high, q_low)):
                    pe.wait_ge(high[p], 1)
                    pe.wait_ge(low[p], 1)
                    for part, t in (("h", hi), ("l", lo)):
                        lhs = sel[side + part][rows, g * HPG:(g + 1) * HPG, :]
                        mm = pe.matmul(bank_b[p][:, i * N:(i + 1) * N],
                                       lhs.rearrange("c h r -> c (h r)"), t[p][rows, :],
                                       start=(part == "h"), stop=(part == "l"))
                mm.then_inc(bc_full[p], 1)

            def score3(s, j, p):
                a_turn(p, ("score", s, j))
                if s == 0 and j < 2:
                    pe.wait_ge(first_keys[p], 1)
                else:
                    pe.wait_ge(km_out[p], 2 * s + j // 2)
                pe.wait_ge(stack_out[p], 2 * s + 2)
                for half in range(2):
                    mm = pe.matmul(bank_a[p][:, half * N:(half + 1) * N],
                                   QKS[p][s % 3][:, 0, half * HALF:(half + 1) * HALF],
                                   KM[p][s % 3][:, j, :], start=True, stop=True)
                mm.then_inc(a_full[p], 1)

            def max_rows(s, p):
                a_turn(p, ("aug", s))
                pe.wait_ge(max_parts[p], s + 1)
                for half in range(2):
                    mm = pe.matmul(bank_a[p][:, half * HALF:(half + 1) * HALF],
                                   AUGW[p][:, half, :], ident_r[:, :], start=True, stop=True)
                mm.then_inc(a_full[p], 1)

            def score_t(s, m, p):
                bc_turn(p, ("score_t", s, m))
                if m == 0:
                    pe.wait_ge(aug_out[p], s + 1)
                for j in range(HPG):
                    mm = pe.matmul(bank_bc[p][:, j * N:(j + 1) * N],
                                   KM[p][s % 3][:, j, m * HALF:(m + 1) * HALF],
                                   QSA[p][:, :], start=True, stop=True)
                mm.then_inc(bc_full[p], 1)

            def mix3(s, m, p):
                b, g = divmod(s, 2)
                pe.wait_ge(exps3[p], 2 * s + m + 1)
                if s > 0:
                    pe.wait_ge(o_out[p], s)
                for j in range(HPG):
                    mm = pe.matmul(bank_d[p][j * QUAD:(j + 1) * QUAD, g * N:(g + 1) * N],
                                   VA[p][b][:, m, g * HPG + j, :], E3[p][s % 2][m][:, j, :],
                                   start=(m == 0), stop=(m == 1))
                if m == 1:
                    mm.then_inc(mixed3[p], 1)

            def turn3(s, p):
                a_turn(p, ("turn", s))
                pe.wait_ge(o_out[p], s + 1)
                for half in range(2):
                    tp = pe.transpose(bank_a[p][:, half * P:(half + 1) * P],
                                      OS[p][:, s % 2, half * HALF:(half + 1) * HALF], ident)
                tp.then_inc(a_full[p], 1)

            def back3(p):
                a_turn(p, ("back",))
                pe.wait_ge(on_out[p], 4)
                for half in range(2):
                    tp = pe.transpose(bank_a[p][:, half * HALF:(half + 1) * HALF],
                                      ON[p][:, half, :, :].rearrange("q b c -> q (b c)"), ident)
                tp.then_inc(a_full[p], 1)

            def out3(p):
                a_turn(p, ("out",))
                pe.wait_ge(ot_out[p], 1)
                pe.matmul(bank_a[p][:, 0:N], w("wp3"), OT[p][:, :], start=True, stop=True)\
                    .then_inc(a_full[p], 1)

            pe.wait_ge(idle_set, 1)
            keep_clock(9, 0)
            project(0, 0)
            keep_clock(3, 0)
            values(0, X[0], 0)
            score(0, 0, 0)
            score(0, 1, 0)
            keep_clock(2, 0)
            project(0, 1)
            turn(0, 0, 0)
            values(0, X[1], 1)
            score(0, 0, 1)
            turn(0, 1, 0)
            score(0, 1, 1)
            mix(0, 0)
            project(1, 0)
            values(1, X[0], 0)
            turn(0, 0, 1)
            turn(0, 1, 1)
            score(1, 0, 0)
            score(1, 1, 0)
            mix(0, 1)
            project(1, 1)
            keep_clock(4, 0)
            values(1, X[1], 1)
            mix(1, 0)
            score(1, 0, 1)
            score(1, 1, 1)
            keep_clock(6, 0)
            project(2, 0)
            values(2, X[0], 0)
            score(2, 0, 0)
            score(2, 1, 0)
            mix(1, 1)
            keep_clock(5, 0)
            project(2, 1)
            turn(2, 0, 0)
            values(2, X[1], 1)
            score(2, 0, 1)
            turn(2, 1, 0)
            score(2, 1, 1)
            mix(2, 0)
            keep_clock(9, 1)
            group_means(0)
            keep_clock(9, 1)
            turn(2, 0, 1)
            turn(2, 1, 1)
            project3(0)
            values(3, XN[0], 0)
            stacks(0, 0)
            mix(2, 1)
            score3(0, 0, 0)
            keep_clock(6, 0)
            group_means(1)
            stacks(1, 0)
            score3(0, 1, 0)
            score3(0, 2, 0)
            project3(1)
            keep_clock(4, 0)
            score3(0, 3, 0)
            values(3, XN[1], 1)
            stacks(0, 1)
            keep_clock(3, 0)
            score3(1, 0, 0)
            score3(0, 0, 1)
            stacks(2, 0)
            max_rows(0, 0)
            stacks(1, 1)
            score3(1, 1, 0)
            score_t(0, 0, 0)
            score3(0, 1, 1)
            score3(1, 2, 0)
            keep_clock(4, 1)
            score3(0, 2, 1)
            score_t(0, 1, 0)
            score3(1, 3, 0)
            stacks(2, 1)
            keep_clock(1, 1)
            score3(0, 3, 1)
            score3(2, 0, 0)
            stacks(3, 0)
            score3(1, 0, 1)
            mix3(0, 0, 0)
            max_rows(1, 0)
            max_rows(0, 1)
            score3(2, 1, 0)
            score_t(1, 0, 0)
            score3(1, 1, 1)
            mix3(0, 1, 0)
            score3(2, 2, 0)
            score_t(0, 0, 1)
            score3(1, 2, 1)
            score3(2, 3, 0)
            score_t(1, 1, 0)
            score3(1, 3, 1)
            score_t(0, 1, 1)
            score3(3, 0, 0)
            mix3(1, 0, 0)
            score3(2, 0, 1)
            stacks(3, 1)
            max_rows(2, 0)
            mix3(0, 0, 1)
            max_rows(1, 1)
            score3(3, 1, 0)
            score_t(2, 0, 0)
            score3(2, 1, 1)
            mix3(1, 1, 0)
            score3(3, 2, 0)
            score_t(1, 0, 1)
            score3(2, 2, 1)
            mix3(0, 1, 1)
            score3(3, 3, 0)
            score_t(2, 1, 0)
            score3(2, 3, 1)
            score_t(1, 1, 1)
            score3(3, 0, 1)
            max_rows(3, 0)
            mix3(2, 0, 0)
            max_rows(2, 1)
            turn3(0, 0)
            score_t(3, 0, 0)
            score3(3, 1, 1)
            score_t(2, 0, 1)
            mix3(2, 1, 0)
            turn3(1, 0)
            score3(3, 2, 1)
            mix3(1, 0, 1)
            score_t(3, 1, 0)
            score3(3, 3, 1)
            mix3(1, 1, 1)
            score_t(2, 1, 1)
            mix3(3, 0, 0)
            max_rows(3, 1)
            mix3(3, 1, 0)
            turn3(2, 0)
            score_t(3, 0, 1)
            turn3(0, 1)
            turn3(3, 0)
            mix3(2, 0, 1)
            mix3(2, 1, 1)
            back3(0)
            turn3(1, 1)
            score_t(3, 1, 1)
            out3(0)
            turn3(2, 1)
            mix3(3, 0, 1)
            mix3(3, 1, 1)
            turn3(3, 1)
            back3(1)
            out3(1)

        @block.scalar
        def _(act):
            def queries(layer, p):
                if layer == 0 and p == 0:
                    act.wait_ge(prep_vector, 1)
                act.wait_ge(q_made[p], layer + 1)
                if layer == 1:
                    act.activation(M1[p][:, :], bank_a[p][:, 0:N], ACT.Identity,
                                   bias=low_bias1[:, :], scale=col("low1")).then_inc(high_out[p], 1)
                    return
                if layer == 0:
                    rows = slice(0, 2 * HID0)
                    act.activation(Qs[p][rows, :], bank_a[p][rows, 0:N], ACT.Identity,
                                   bias=col("b0")[rows, :]).then_inc(q_out[p], 1)
                    act.wait_ge(prep_pool, p + 1)
                    rows = slice(3 * HID0, 4 * HID0)
                    act.activation(K0s[p][HID0:2 * HID0, 1, :], bank_a[p][rows, 0:N], ACT.Identity,
                                   bias=col("b0")[rows, :]).then_inc(k_out1[p], 1)
                else:
                    rows = slice(C, P)
                    act.activation(Qs[p][:, :], bank_a[p][:, 0:N], ACT.Copy).then_inc(q_out[p], 1)
                    act.wait_ge(k_made[p], 1)
                    act.wait_ge(prep_pool, 2 * PAIRS)
                    act.activation(Ks[p][rows, 1, :], bank_b[p][rows, 0:N], ACT.Copy)\
                        .then_inc(k_out1[p], 1)

            def values2(p):
                act.wait_ge(v_made[p], 3)
                act.activation(V[p][:, :, :].rearrange("t h c -> t (h c)"), bank_c[p][:, 0:N],
                               ACT.Copy).then_inc(v_out[p], 1)

            def exponents(layer, b, p):
                bank = (bank_a, bank_b)[b][p]
                act.wait_ge(maxima[p], 2 * layer + b + 1)
                for half in range(2):
                    e = act.activation(E[p][b][:, half, :], bank[:, half * N:(half + 1) * N],
                                       ACT.Exp, bias=NM[p][b][:, half:half + 1],
                                       accum_out=SUM[p][b][:, half:half + 1])
                e.then_inc(exps[p], 1)

            def turned_copy(layer, p):
                act.wait_ge(turned[p], 2 * (layer // 2) + 1)
                act.activation(ET[p][0][:, :, :].rearrange("m h n -> m (h n)"), bank_a[p][:, :],
                               ACT.Copy).then_inc(turned_out[p], 1)

            def high_parts(p):
                act.wait_ge(k_made[p], 2)
                act.wait_ge(stat[p], 9)
                act.activation(KH[p][:, :], bank_b[p][:, 0:N], ACT.Identity, bias=GM[p][:, 2:3])\
                    .then_inc(k_high[p], 1)
                act.wait_ge(q_made[p], 4)
                act.activation(QH[p][:, :], bank_a[p][:, 0:N], ACT.Identity, bias=col("bq3"))\
                    .then_inc(q_high[p], 1)

            def stack_copy(s, p):
                act.wait_ge(bc_full[p], BC_ITEM[("stacks", s)] + 1)
                if s >= 3:
                    act.wait_ge(bc_full[p], BC_ITEM[("score_t", s - 3, 1)] + 1)
                act.activation(QKS[p][s % 3][:, 1, :], bank_b[p][:, N:2 * N], ACT.Identity,
                               bias=col("ones_rows")).then_inc(stack_out[p], 1)
                act.activation(QKS[p][s % 3][:, 0, :], bank_b[p][:, 0:N], ACT.Copy)\
                    .then_inc(stack_out[p], 1)

            def exps_t(s, m, p):
                act.wait_ge(bc_full[p], BC_ITEM[("score_t", s, m)] + 1)
                if s >= 2:
                    act.wait_ge(mixed3[p], s - 1)
                act.activation(E3[p][s % 2][m][:, :, :].rearrange("k j q -> k (j q)"),
                               bank_bc[p][:, :], ACT.Exp, scale=float(HD) ** -0.5)\
                    .then_inc(exps3[p], 1)

            def o_copy(s, p):
                act.wait_ge(mixed3[p], s + 1)
                if s >= 2:
                    act.wait_ge(a_full[p], A_ITEM[("turn", s - 2)] + 1)
                act.activation(OS[p][:, s % 2, :], bank_d[p][:, s % 2 * N:(s % 2 + 1) * N],
                               ACT.Copy).then_inc(o_out[p], 1)

            def ot_copy(p):
                act.wait_ge(a_full[p], A_ITEM[("back",)] + 1)
                act.activation(OT[p][:, :], bank_a[p][:, 0:N], ACT.Copy).then_inc(ot_out[p], 1)

            for g in (0, VALUES0):
                a, z = spans[g]
                act.dma_start(W[:, a:z], pack[:, a:z]).then_inc(w_loaded[g], 16)
            act.preload_act_table(ACT.Exp)
            queries(0, 0)
            exponents(0, 0, 0)
            queries(0, 1)
            exponents(0, 1, 0)
            turned_copy(0, 0)
            exponents(0, 0, 1)
            exponents(0, 1, 1)
            queries(1, 0)
            turned_copy(0, 1)
            exponents(1, 0, 0)
            exponents(1, 1, 0)
            queries(1, 1)
            exponents(1, 0, 1)
            queries(2, 0)
            exponents(1, 1, 1)
            exponents(2, 0, 0)
            values2(0)
            exponents(2, 1, 0)
            queries(2, 1)
            values2(1)
            turned_copy(2, 0)
            exponents(2, 0, 1)
            exponents(2, 1, 1)
            turned_copy(2, 1)
            high_parts(0)
            stack_copy(0, 0)
            high_parts(1)
            stack_copy(1, 0)
            stack_copy(0, 1)
            stack_copy(2, 0)
            stack_copy(1, 1)
            exps_t(0, 0, 0)
            exps_t(0, 1, 0)
            stack_copy(2, 1)
            stack_copy(3, 0)
            exps_t(1, 0, 0)
            o_copy(0, 0)
            exps_t(0, 0, 1)
            exps_t(0, 1, 1)
            exps_t(1, 1, 0)
            stack_copy(3, 1)
            exps_t(2, 0, 0)
            exps_t(1, 0, 1)
            o_copy(0, 1)
            exps_t(2, 1, 0)
            o_copy(1, 0)
            exps_t(1, 1, 1)
            exps_t(3, 0, 0)
            o_copy(2, 0)
            exps_t(2, 0, 1)
            exps_t(3, 1, 0)
            o_copy(1, 1)
            exps_t(2, 1, 1)
            o_copy(3, 0)
            exps_t(3, 0, 1)
            o_copy(2, 1)
            ot_copy(0)
            exps_t(3, 1, 1)
            o_copy(3, 1)
            ot_copy(1)

        @block.vector
        def _(dve):
            dve.memset(idle[:, :].bitcast(f32), 0.0).then_inc(idle_set, 1)
            dve.wait_ge(w_loaded[0], 16)
            dve.tensor_tensor(low_bias1[:, :], col("b1"), col("low1"), ALU.mult)\
                .then_inc(prep_vector, 1)
            for i, name in enumerate(("bk3", "proj_b")):
                dve.scalar_tensor_tensor(feature_bias[:, i:i + 1], col("gproj_b"), 0.1, col(name),
                                         ALU.mult, ALU.add).then_inc(prep_vector, 1)

            def keys(layer, p):
                if layer == 1:
                    dve.wait_ge(high_out[p], 1)
                    for dst, rows, done in ((F1, slice(0, C), q_out), (G1, slice(C, P), k_out)):
                        dve.scalar_tensor_tensor(dst[p][:, :], bank_a[p][rows, 0:N],
                                                 col("b1")[rows, :], M1[p][rows, :].bitcast(f32),
                                                 ALU.add, ALU.subtract).then_inc(done[p], 1)
                    return
                if layer == 0:
                    rows = slice(2 * HID0, 3 * HID0)
                    dve.wait_ge(q_made[p], 1)
                    dve.wait_ge(prep_pool, p + 1)
                    dve.tensor_scalar(K0s[p][0:HID0, 0, :], bank_a[p][rows, 0:N],
                                      col("b0")[rows, :], None, ALU.add).then_inc(k_out[p], 1)
                else:
                    rows = slice(0, C)
                    dve.wait_ge(k_made[p], 1)
                    dve.wait_ge(prep_pool, 2 * PAIRS)
                    dve.tensor_copy(Ks[p][rows, 0, :], bank_b[p][rows, 0:N]).then_inc(k_out[p], 1)

            def add_value_bias(layer, p):
                if layer == 0 and p == 0:
                    dve.wait_ge(w_loaded[VALUES0], 16)
                dve.wait_ge(v_made[p], layer + 1)
                bias = w(f"vb{layer}").unsqueeze(1).broadcast_to([P, 2, P])
                dve.tensor_tensor(V[p][:, :, :], bank_c[p][:, 0:N].rearrange(
                    "t (h c) -> t h c", h=2), bias, ALU.add).then_inc(v_out[p], 1)

            def row_maxima(layer, b, p):
                bank = (bank_a, bank_b)[b][p]
                dve.wait_ge(scores[p], 2 * layer + b + 1)
                dve.tensor_reduce(NM[p][b][:, :], bank.rearrange("r (h c) -> r h c", h=2), AX.X,
                                  ALU.max, negate=True).then_inc(maxima[p], 1)

            def divide(layer, b, p):
                i = 2 * layer + b
                dve.wait_ge(exps[p], i + 1)
                dve.reciprocal(RS[p][b][:, :], SUM[p][b][:, :]).then_inc(recips[p], 1)
                dve.wait_ge(recips[p], i + 1)
                if layer == 1:
                    cols = slice(b * C, (b + 1) * C)
                    dve.wait_ge(v_out[p], 2)
                    dve.tensor_tensor(VS[p][:, :, cols], V[p][:, :, cols],
                                      RS[p][b][:, :].unsqueeze(2).broadcast_to([P, 2, C]),
                                      ALU.mult).then_inc(divided[p], 1)
                else:
                    for half in range(2):
                        d = dve.tensor_scalar(E[p][b][:, half, :], E[p][b][:, half, :],
                                              RS[p][b][:, half:half + 1], None, ALU.mult)
                    d.then_inc(divided[p], 1)

            def turned_copy(layer, p):
                dve.wait_ge(turned[p], 2 * (layer // 2) + 2)
                dve.tensor_copy(ET[p][1][:, :, :].rearrange("m h n -> m (h n)"), bank_b[p][:, :])\
                    .then_inc(turned_out1[p], 1)

            def residual(layer, p):
                dve.wait_ge(mixed[p], layer + 1)
                if layer == 0:
                    dve.tensor_tensor(X[p][:, :], bank_c[p][:, 0:N], X[p][:, :], ALU.add)\
                        .then_inc(x_new[p], 1)
                else:
                    dve.scalar_tensor_tensor(X[p][:, :], bank_c[p][:, 0:N], col(f"gamma{layer}"),
                                             X[p][:, :], ALU.mult, ALU.add).then_inc(x_new[p], 1)

            def small(p, n, ins):
                ins.then_inc(stat[p], 1)
                dve.wait_ge(stat[p], n)

            def statistics(p):
                dve.wait_ge(x_new[p], 3)
                small(p, 1, dve.bn_stats(ST6[p][:, :], X[p][:, :]))
                small(p, 2, dve.bn_aggr(MV[p][:, :], ST6[p][:, :]))

            def group_variance(p):
                m = GM[p]
                dve.wait_ge(group_mean[p], 1)
                dve.tensor_tensor(m[:, 0:1], MV[p][:, 0:1], bank_d[p][:, 0:1], ALU.subtract)\
                    .then_inc(stat[p], 1)
                small(p, 4, dve.tensor_scalar(m[:, 7:8], bank_d[p][:, 1:2], EPS, None, ALU.add))
                small(p, 5, dve.scalar_tensor_tensor(m[:, 2:3], m[:, 0:1], m[:, 0:1], m[:, 7:8],
                                                     ALU.mult, ALU.add))

            def normalise(p):
                m = GM[p]
                dve.wait_ge(rstd[p], 1)
                small(p, 6, dve.tensor_tensor(m[:, 4:5], m[:, 3:4], col("gn_w"), ALU.mult))
                small(p, 7, dve.scalar_tensor_tensor(m[:, 5:6], bank_d[p][:, 0:1], m[:, 4:5],
                                                     col("gn_b"), ALU.mult, ALU.subtract))
                dve.scalar_tensor_tensor(m[:, 6:7], MV[p][:, 0:1], m[:, 4:5], m[:, 5:6],
                                         ALU.mult, ALU.subtract).then_inc(stat[p], 1)
                dve.tensor_scalar(XN[p][:, :], X[p][:, :], m[:, 4:5], m[:, 5:6], ALU.mult,
                                  ALU.subtract).then_inc(xn_out[p], 1)

            def global_feature(p):
                m = GM[p]
                dve.wait_ge(gfeat_made[p], 1)
                if p == 0:
                    dve.wait_ge(prep_vector, 3)
                for column, i in ((2, 0), (1, 1)):
                    dve.scalar_tensor_tensor(m[:, column:column + 1], bank_d[p][:, 0:1], 0.1,
                                             feature_bias[:, i:i + 1], ALU.mult, ALU.add)\
                        .then_inc(stat[p], 1)

            def low_queries(p):
                dve.wait_ge(q_high[p], 1)
                dve.scalar_tensor_tensor(QL[p][:, :], bank_a[p][:, 0:N], col("bq3"),
                                         QH[p][:, :].bitcast(f32), ALU.add, ALU.subtract)\
                    .then_inc(q_low[p], 1)

            def low_keys(p):
                dve.wait_ge(k_high[p], 1)
                dve.scalar_tensor_tensor(KL[p][:, :], bank_b[p][:, 0:N], GM[p][:, 2:3],
                                         KH[p][:, :].bitcast(f32), ALU.add, ALU.subtract)\
                    .then_inc(k_low[p], 1)

            def values3(p):
                dve.wait_ge(v_made[p], 4)
                if p == 0:
                    dve.wait_ge(prep_pool, PREPARED)
                for b in range(2):
                    src = bank_c[p][:, 0:N].rearrange("t (h b e d) -> t h b e d", h=2, b=2, d=HD)
                    bias = w("vb3")[:, 0:C].rearrange("t (e d) -> t e d", d=HD)
                    bias = bias.unsqueeze(1).broadcast_to([P, 2, HEADS, HD])
                    v = dve.tensor_tensor(VA[p][b][:, :, :, 0:HD], src[:, :, b], bias, ALU.add)
                v.then_inc(v_out[p], 1)

            def first_head_keys(p):
                dve.wait_ge(stack_out[p], 1)
                for j in range(2):
                    k = dve.tensor_scalar(KM[p][0][:, j, :], QKS[p][0][:, 1, :].bitcast(f32),
                                          w("heads")[:, j:j + 1], None, ALU.mult)
                k.then_inc(first_keys[p], 1)

            def maxima_of(s, j, p):
                dve.wait_ge(a_full[p], A_ITEM[("score", s, j)] + 1)
                dve.tensor_reduce(NM3[p][:, s % 2, :, j],
                                  bank_a[p].rearrange("q (h k) -> q h k", h=2),
                                  AX.X, ALU.max, negate=True).then_inc(maxima3[p], 1)

            def rows_of_maxima(p):
                return AUGW[p][:, :, :].rearrange("q h (j r) -> q h j r", r=QUAD)

            def high_of_maxima(s, p):
                dve.wait_ge(maxima3[p], 4 * s + 4)
                dve.tensor_copy(rows_of_maxima(p)[:, :, :, MAXROW], NM3[p][:, s % 2, :, :])\
                    .then_inc(max_high[p], 1)

            def low_of_maxima(s, p):
                dve.wait_ge(max_high[p], s + 1)
                dve.tensor_tensor(rows_of_maxima(p)[:, :, :, MAXROW + 1], NM3[p][:, s % 2, :, :],
                                  rows_of_maxima(p)[:, :, :, MAXROW].bitcast(f32), ALU.subtract)\
                    .then_inc(max_parts[p], 1)

            def add_max_rows(s, p):
                dve.wait_ge(a_full[p], A_ITEM[("aug", s)] + 1)
                if s > 0:
                    dve.wait_ge(bc_full[p], BC_ITEM[("score_t", s - 1, 1)] + 1)
                dve.tensor_tensor(QSA[p][:, :], QKS[p][s % 3][:, 0, :].bitcast(f32),
                                  bank_a[p][:, 0:N], ALU.add)\
                    .then_inc(aug_out[p], 1)

            def divide3(s, p):
                b, g = divmod(s, 2)
                dve.wait_ge(a_full[p], A_ITEM[("turn", s)] + 1)
                src = bank_a[p][:, 0:N].rearrange("q (h j r) -> q h j r", h=2, r=QUAD)
                dve.reciprocal(R3[p][:, s, :, :], src[:, :, :, HD]).then_inc(recips3[p], 1)
                dve.wait_ge(recips3[p], s + 1)
                to = ON[p][:, :, b, :].rearrange("q h (i j d) -> q h i j d", i=2, d=HD)
                dve.tensor_tensor(to[:, :, g], src[:, :, :, 0:HD],
                                  R3[p][:, s, :, :].unsqueeze(3).broadcast_to([P, 2, HPG, HD]),
                                  ALU.mult).then_inc(on_out[p], 1)

            def result(p):
                dve.wait_ge(a_full[p], A_ITEM[("out",)] + 1)
                dve.scalar_tensor_tensor(Y[p][:, :], bank_a[p][:, 0:N], GM[p][:, 1:2], X[p][:, :],
                                         ALU.add, ALU.add).then_inc(y_out[p], 1)

            keys(0, 0)
            add_value_bias(0, 0)
            row_maxima(0, 0, 0)
            row_maxima(0, 1, 0)
            divide(0, 0, 0)
            keys(0, 1)
            divide(0, 1, 0)
            add_value_bias(0, 1)
            turned_copy(0, 0)
            row_maxima(0, 0, 1)
            row_maxima(0, 1, 1)
            residual(0, 0)
            divide(0, 0, 1)
            divide(0, 1, 1)
            add_value_bias(1, 0)
            keys(1, 0)
            turned_copy(0, 1)
            row_maxima(1, 0, 0)
            row_maxima(1, 1, 0)
            residual(0, 1)
            divide(1, 0, 0)
            divide(1, 1, 0)
            keys(1, 1)
            add_value_bias(1, 1)
            residual(1, 0)
            row_maxima(1, 0, 1)
            row_maxima(1, 1, 1)
            keys(2, 0)
            divide(1, 0, 1)
            divide(1, 1, 1)
            row_maxima(2, 0, 0)
            row_maxima(2, 1, 0)
            residual(1, 1)
            divide(2, 0, 0)
            keys(2, 1)
            divide(2, 1, 0)
            turned_copy(2, 0)
            row_maxima(2, 0, 1)
            row_maxima(2, 1, 1)
            residual(2, 0)
            statistics(0)
            divide(2, 0, 1)
            group_variance(0)
            divide(2, 1, 1)
            normalise(0)
            global_feature(0)
            turned_copy(2, 1)
            low_keys(0)
            low_queries(0)
            first_head_keys(0)
            residual(2, 1)
            statistics(1)
            maxima_of(0, 0, 0)
            values3(0)
            group_variance(1)
            maxima_of(0, 1, 0)
            normalise(1)
            global_feature(1)
            maxima_of(0, 2, 0)
            low_keys(1)
            low_queries(1)
            maxima_of(0, 3, 0)
            values3(1)
            first_head_keys(1)
            high_of_maxima(0, 0)
            maxima_of(1, 0, 0)
            low_of_maxima(0, 0)
            maxima_of(0, 0, 1)
            add_max_rows(0, 0)
            maxima_of(1, 1, 0)
            maxima_of(0, 1, 1)
            maxima_of(1, 2, 0)
            maxima_of(0, 2, 1)
            maxima_of(1, 3, 0)
            high_of_maxima(1, 0)
            maxima_of(0, 3, 1)
            low_of_maxima(1, 0)
            high_of_maxima(0, 1)
            maxima_of(2, 0, 0)
            low_of_maxima(0, 1)
            maxima_of(1, 0, 1)
            add_max_rows(1, 0)
            add_max_rows(0, 1)
            maxima_of(2, 1, 0)
            maxima_of(1, 1, 1)
            maxima_of(2, 2, 0)
            maxima_of(1, 2, 1)
            maxima_of(2, 3, 0)
            maxima_of(1, 3, 1)
            high_of_maxima(2, 0)
            low_of_maxima(2, 0)
            high_of_maxima(1, 1)
            maxima_of(3, 0, 0)
            low_of_maxima(1, 1)
            maxima_of(2, 0, 1)
            add_max_rows(2, 0)
            add_max_rows(1, 1)
            maxima_of(3, 1, 0)
            maxima_of(2, 1, 1)
            maxima_of(3, 2, 0)
            maxima_of(2, 2, 1)
            maxima_of(3, 3, 0)
            maxima_of(2, 3, 1)
            high_of_maxima(2, 1)
            high_of_maxima(3, 0)
            low_of_maxima(2, 1)
            low_of_maxima(3, 0)
            maxima_of(3, 0, 1)
            add_max_rows(3, 0)
            add_max_rows(2, 1)
            divide3(0, 0)
            maxima_of(3, 1, 1)
            maxima_of(3, 2, 1)
            maxima_of(3, 3, 1)
            high_of_maxima(3, 1)
            divide3(1, 0)
            low_of_maxima(3, 1)
            add_max_rows(3, 1)
            divide3(2, 0)
            divide3(0, 1)
            divide3(3, 0)
            divide3(1, 1)
            divide3(2, 1)
            result(0)
            divide3(3, 1)
            result(1)


def packed(i):
    where, _, width = places()
    pack = np.zeros((P, width), np.float32)

    def put(name, t):
        a, n = where[name]
        pack[:t.shape[0], a:a + t.shape[1]] = t

    def both(name, wt):
        a, _ = where[name]
        for b in range(2):
            pack[b * C:(b + 1) * C, a + b * C:a + b * C + wt.shape[1]] = wt

    def column(name, v):
        pack[:, where["cols"][0] + COLS.index(name)] = v

    for side, name in enumerate(("L0_conv_Wq", "L0_conv_Wk")):
        for b in range(2):
            at = where["w0"][0] + (2 * side + b) * HID0
            pack[b * C:(b + 1) * C, at:at + HID0] = i[name].T
    both("wv0", i["L0_conv_Wv"].T)
    both("wv1", i["L1_conv_Wh"].T)
    both("wq2", i["L2_conv_Wq"].T)
    both("wk2", i["L2_conv_Wk"].T)
    both("wv2", i["L2_conv_Wv"].T)
    qkv, qkv_b = i["L3_conv_qkv_w"], i["L3_conv_qkv_b"]
    both("wq3", qkv[0:C].T)
    both("wk3", qkv[C:2 * C].T)
    both("wv3", qkv[2 * C:3 * C].T)
    both("wg3", i["L3_conv_gproj_w"].T)
    both("wp3", i["L3_conv_proj_w"].T)
    a, _ = where["w1"]
    for side, name in enumerate(("L1_conv_Wf", "L1_conv_Wg")):
        for b in range(2):
            at = a + side * C + b * KINDS1 * HID1
            pack[b * C:(b + 1) * C, at:at + KINDS1 * HID1] = np.tile(i[name].T, (1, KINDS1))
    for name, v in (("vb0", i["L0_conv_bv"]), ("vb1", i["L1_conv_bh"]), ("vb3", qkv_b[2 * C:])):
        put(name, np.tile(v, (P, 2)))
    column("b0", np.concatenate([np.tile(i["L0_conv_bq"], 2), np.tile(i["L0_conv_bk"], 2)]))
    column("b1", np.concatenate([np.tile(i["L1_conv_bf"], 2 * KINDS1),
                                 np.tile(i["L1_conv_bg"], 2 * KINDS1)]))
    column("gamma1", i["L1_conv_gamma"][0])
    column("gamma2", i["L2_conv_gamma"][0])
    column("bq3", np.tile(qkv_b[0:C], 2))
    column("bk3", np.tile(qkv_b[C:2 * C], 2))
    for name, v in (("gn_w", i["L3_conv_gn_w"]), ("gn_b", i["L3_conv_gn_b"]),
                    ("proj_b", i["L3_conv_proj_b"]), ("gproj_b", i["L3_conv_gproj_b"])):
        column(name, np.tile(v, 2))
    rows = np.arange(P)
    column("low1", np.concatenate([np.isin(rows[:C] // HID1 % KINDS1, Q_LOW),
                                   np.isin(rows[:C] // HID1 % KINDS1, K_LOW)]))
    column("ones_rows", (rows % QUAD == MAXROW) | (rows % QUAD == MAXROW + 1))
    put("heads", rows[:, None] // QUAD == np.arange(HPG))
    put("ident", np.eye(P))
    put("fold", np.eye(C)[rows % C])
    put("gavg", (rows[:, None] // GROUP == rows[None, :] // GROUP) / GROUP)
    return pack


def kernel(**inputs):
    import concourse.bacc as bacc
    from concourse.bass_utils import run_bass_kernel_spmd

    inputs = {k: np.asarray(v) for k, v in inputs.items()}
    arrays = {"x": np.ascontiguousarray(inputs["x"]), "pack": packed(inputs)}
    nc = bacc.Bacc("TRN2", target_bir_lowering=False, num_devices=1)
    args = [nc.dram_tensor(n, a.shape, mybir.dt.from_np(a.dtype), kind="ExternalInput").ap()
            for n, a in arrays.items()]
    args.append(nc.dram_tensor("out", (B, C, 16, 16), mybir.dt.float32, kind="ExternalOutput").ap())
    conv_attention_chain(nc, *args)
    return run_bass_kernel_spmd(nc, [arrays], core_ids=[0]).results[0]["out"]
```
